# Optimizing a Trainium2 kernel written in Bass

```python
import numpy as np
import jax
import jax.numpy as jnp

def _softmax(x, axis=-1):
    return jax.nn.softmax(x, axis=axis)

def _gelu(x):
    return jax.nn.gelu(x, approximate=True)

def _silu(x):
    return jax.nn.silu(x)

def _sigmoid(x):
    return jax.nn.sigmoid(x)

def _layernorm(x, axis=-1, eps=1e-05):
    m = jnp.mean(x, axis=axis, keepdims=True)
    v = jnp.var(x, axis=axis, keepdims=True)
    return (x - m) / jnp.sqrt(v + eps)

def _scatter_add(tgt, idx, src, axis=0):
    return tgt.at[idx].add(src)

def _segment_sum(src, seg, n):
    return jax.ops.segment_sum(src, seg, n)
kernel_name = 'mk_adj_seq_d4_adj_r2_401369'

def setup_inputs(seed: int=0):
    np.random.seed(seed)
    _w = jnp.asarray

    def _rec_inputs():
        import jax
        import jax.numpy as jnp
        _gk = jax.random.key(seed)
        x = -0.0005207 + 1.001 * jax.random.normal(jax.random.fold_in(_gk, 1), (64, 128, 256), jnp.float32)
        _a = jax.random.bernoulli(jax.random.fold_in(_gk, 2), 0.125, (64, 128, 128))
        _a = jnp.logical_or(_a, jnp.swapaxes(_a, -1, -2))
        _a = jnp.logical_or(_a, jnp.eye(128, dtype=bool))
        _af = _a.astype(jnp.float32)
        _af = _af * jax.random.uniform(jax.random.fold_in(_gk, 3), (64, 128, 128), jnp.float32, 0.05, 1)
        adj = _af
        return (x, adj)
    x, adj = _rec_inputs()

    def _L0_gnn_setup():
        import jax, jax.numpy as jnp
        import numpy as np
        NUM_HEADS = 8
        EPS = 1e-09
        key = jax.random.key(seed)
        ks = jax.random.split(key, 8)
        B, N, D = (2, 1024, 256)
        s = 1.0 / np.sqrt(D)
        x = jax.random.normal(ks[0], (B, N, D), dtype=jnp.float32)
        adjacency = jax.random.uniform(ks[1], (B, N, N), dtype=jnp.float32)
        W_q = jax.random.normal(ks[2], (D, D), dtype=jnp.float32) * s
        W_k = jax.random.normal(ks[3], (D, D), dtype=jnp.float32) * s
        W_v = jax.random.normal(ks[4], (D, D), dtype=jnp.float32) * s
        b_q = jnp.zeros((D,), jnp.float32)
        b_k = jnp.zeros((D,), jnp.float32)
        b_v = jnp.zeros((D,), jnp.float32)
        w_g = jax.random.normal(ks[5], (2 * D,), dtype=jnp.float32) * (1.0 / np.sqrt(2 * D))
        b_g = jnp.zeros((), jnp.float32)
        return {'x': x, 'adjacency': adjacency, 'W_q': W_q, 'b_q': b_q, 'W_k': W_k, 'b_k': b_k, 'W_v': W_v, 'b_v': b_v, 'w_g': w_g, 'b_g': b_g}
    _L0_gnn_all = _L0_gnn_setup()
    _L0_gnn_in = {k: v for k, v in _L0_gnn_all.items() if k in ('W_q', 'b_q', 'W_k', 'b_k', 'W_v', 'b_v', 'w_g', 'b_g')}
    del _L0_gnn_all

    def _L1_gnn_setup():
        import jax, jax.numpy as jnp
        import numpy as np
        import math
        EMBED = 256
        DFF = 256
        B, N = (8, 1024)
        key = jax.random.key(seed)
        ks = jax.random.split(key, 8)
        node_fts = jax.random.normal(ks[0], (B, N, EMBED), dtype=jnp.float32)
        rel_edges = jax.random.randint(ks[1], (B, N, N), 0, 2).astype(jnp.float32)
        s = 1.0 / math.sqrt(EMBED)
        Wq = jax.random.normal(ks[2], (EMBED, DFF), dtype=jnp.float32) * s
        bq = jnp.zeros((DFF,), dtype=jnp.float32)
        Wk = jax.random.normal(ks[3], (EMBED, DFF), dtype=jnp.float32) * s
        bk = jnp.zeros((DFF,), dtype=jnp.float32)
        Wc = jax.random.normal(ks[4], (EMBED, EMBED), dtype=jnp.float32) * s
        gamma = jnp.ones((EMBED,), dtype=jnp.float32)
        beta = jnp.zeros((EMBED,), dtype=jnp.float32)
        return {'node_fts': node_fts, 'rel_edges': rel_edges, 'Wq': Wq, 'bq': bq, 'Wk': Wk, 'bk': bk, 'Wc': Wc, 'gamma': gamma, 'beta': beta}
    _L1_gnn_all = _L1_gnn_setup()
    _L1_gnn_in = {k: v for k, v in _L1_gnn_all.items() if k in ('Wq', 'bq', 'Wk', 'bk', 'Wc', 'gamma', 'beta')}
    del _L1_gnn_all

    def _L2_gnn_setup():
        import jax, jax.numpy as jnp
        import numpy as np
        BS, N, H = (8, 1024, 256)
        NEG_INF = -1000000000.0
        LEAKY_SLOPE = 0.01
        key = jax.random.key(seed)
        ks = jax.random.split(key, 8)
        feats = jax.random.normal(ks[0], (BS, N, H), dtype=jnp.float32)
        adj = jax.random.randint(ks[1], (BS, N, N), 0, 2).astype(jnp.float32)
        adj = jnp.maximum(adj, jnp.eye(N, dtype=jnp.float32)[None])
        s = 1.0 / np.sqrt(H)
        return {'feats': feats, 'adj_mat': adj, 'fc_w': jax.random.normal(ks[2], (H, H), dtype=jnp.float32) * s, 'fc_b': jax.random.normal(ks[3], (H,), dtype=jnp.float32) * s, 'q_w': jax.random.normal(ks[4], (1, H), dtype=jnp.float32) * s, 'q_b': jax.random.normal(ks[5], (1,), dtype=jnp.float32) * s, 'k_w': jax.random.normal(ks[6], (1, H), dtype=jnp.float32) * s, 'k_b': jax.random.normal(ks[7], (1,), dtype=jnp.float32) * s}
    _L2_gnn_all = _L2_gnn_setup()
    _L2_gnn_in = {k: v for k, v in _L2_gnn_all.items() if k in ('fc_w', 'fc_b', 'q_w', 'q_b', 'k_w', 'k_b')}
    del _L2_gnn_all

    def _L3_gnn_setup():
        import jax, jax.numpy as jnp
        import numpy as np
        B, N, D, H = (8, 512, 256, 8)
        DK = D // H
        LN_EPS = 1e-05
        ADJ_MIN = 1e-08

        def _layer_norm(x, gamma, beta):
            mu = jnp.mean(x, axis=-1, keepdims=True)
            var = jnp.mean(jnp.square(x - mu), axis=-1, keepdims=True)
            return (x - mu) * jax.lax.rsqrt(var + LN_EPS) * gamma + beta
        key = jax.random.key(seed)
        ks = jax.random.split(key, 12)
        x = jax.random.normal(ks[0], (B, N, D), dtype=jnp.float32)
        adj = jax.random.uniform(ks[1], (B, N, N), dtype=jnp.float32)
        adj = adj / jnp.sum(adj, axis=-1, keepdims=True)
        s = 1.0 / np.sqrt(D)
        Wq = jax.random.normal(ks[2], (D, D), dtype=jnp.float32) * s
        bq = jnp.zeros((D,), dtype=jnp.float32)
        Wk = jax.random.normal(ks[3], (D, D), dtype=jnp.float32) * s
        bk = jnp.zeros((D,), dtype=jnp.float32)
        Wv = jax.random.normal(ks[4], (D, D), dtype=jnp.float32) * s
        bv = jnp.zeros((D,), dtype=jnp.float32)
        Wo = jax.random.normal(ks[5], (D, D), dtype=jnp.float32) * s
        bo = jnp.zeros((D,), dtype=jnp.float32)
        gamma = jnp.ones((D,), dtype=jnp.float32)
        beta = jnp.zeros((D,), dtype=jnp.float32)
        return {'x': x, 'adj': adj, 'Wq': Wq, 'bq': bq, 'Wk': Wk, 'bk': bk, 'Wv': Wv, 'bv': bv, 'Wo': Wo, 'bo': bo, 'gamma': gamma, 'beta': beta}
    _L3_gnn_all = _L3_gnn_setup()
    _L3_gnn_in = {k: v for k, v in _L3_gnn_all.items() if k in ('Wq', 'bq', 'Wk', 'bk', 'Wv', 'bv', 'Wo', 'bo', 'gamma', 'beta')}
    del _L3_gnn_all
    return {'x': x, 'adj': adj, 'L0_gnn_W_q': _L0_gnn_in['W_q'], 'L0_gnn_b_q': _L0_gnn_in['b_q'], 'L0_gnn_W_k': _L0_gnn_in['W_k'], 'L0_gnn_b_k': _L0_gnn_in['b_k'], 'L0_gnn_W_v': _L0_gnn_in['W_v'], 'L0_gnn_b_v': _L0_gnn_in['b_v'], 'L0_gnn_w_g': _L0_gnn_in['w_g'], 'L0_gnn_b_g': _L0_gnn_in['b_g'], 'L1_gnn_Wq': _L1_gnn_in['Wq'], 'L1_gnn_bq': _L1_gnn_in['bq'], 'L1_gnn_Wk': _L1_gnn_in['Wk'], 'L1_gnn_bk': _L1_gnn_in['bk'], 'L1_gnn_Wc': _L1_gnn_in['Wc'], 'L1_gnn_gamma': _L1_gnn_in['gamma'], 'L1_gnn_beta': _L1_gnn_in['beta'], 'L2_gnn_fc_w': _L2_gnn_in['fc_w'], 'L2_gnn_fc_b': _L2_gnn_in['fc_b'], 'L2_gnn_q_w': _L2_gnn_in['q_w'], 'L2_gnn_q_b': _L2_gnn_in['q_b'], 'L2_gnn_k_w': _L2_gnn_in['k_w'], 'L2_gnn_k_b': _L2_gnn_in['k_b'], 'L3_gnn_Wq': _L3_gnn_in['Wq'], 'L3_gnn_bq': _L3_gnn_in['bq'], 'L3_gnn_Wk': _L3_gnn_in['Wk'], 'L3_gnn_bk': _L3_gnn_in['bk'], 'L3_gnn_Wv': _L3_gnn_in['Wv'], 'L3_gnn_bv': _L3_gnn_in['bv'], 'L3_gnn_Wo': _L3_gnn_in['Wo'], 'L3_gnn_bo': _L3_gnn_in['bo'], 'L3_gnn_gamma': _L3_gnn_in['gamma'], 'L3_gnn_beta': _L3_gnn_in['beta']}

def reference(x, adj, L0_gnn_W_q, L0_gnn_b_q, L0_gnn_W_k, L0_gnn_b_k, L0_gnn_W_v, L0_gnn_b_v, L0_gnn_w_g, L0_gnn_b_g, L1_gnn_Wq, L1_gnn_bq, L1_gnn_Wk, L1_gnn_bk, L1_gnn_Wc, L1_gnn_gamma, L1_gnn_beta, L2_gnn_fc_w, L2_gnn_fc_b, L2_gnn_q_w, L2_gnn_q_b, L2_gnn_k_w, L2_gnn_k_b, L3_gnn_Wq, L3_gnn_bq, L3_gnn_Wk, L3_gnn_bk, L3_gnn_Wv, L3_gnn_bv, L3_gnn_Wo, L3_gnn_bo, L3_gnn_gamma, L3_gnn_beta):
    import jax
    import jax.numpy as jnp

    def _L0_gnn_ref(x, adjacency, W_q, b_q, W_k, b_k, W_v, b_v, w_g, b_g):
        import jax, jax.numpy as jnp
        import numpy as np
        NUM_HEADS = 8
        EPS = 1e-09
        B, N, D = x.shape
        H = NUM_HEADS
        hd = D // H
        Q = (x @ W_q + b_q).reshape(B, N, H, hd)
        K = (x @ W_k + b_k).reshape(B, N, H, hd)
        V = (x @ W_v + b_v).reshape(B, N, H, hd)
        scores = jnp.einsum('bihd,bjhd->bhij', Q, K) / jnp.sqrt(jnp.float32(hd))
        a = x @ w_g[:D]
        c = x @ w_g[D:]
        soul_bias = a[:, :, None] + c[:, None, :] + b_g
        scores = scores + (soul_bias + jnp.log(adjacency + EPS))[:, None, :, :]
        attn = jax.nn.softmax(scores, axis=-1)
        out = jnp.einsum('bhij,bjhd->bihd', attn, V).reshape(B, N, D)
        return out + x

    def _L1_gnn_ref(node_fts, rel_edges, Wq, bq, Wk, bk, Wc, gamma, beta):
        import jax, jax.numpy as jnp
        import numpy as np
        import math
        EMBED = 256
        DFF = 256
        B, N = (8, 1024)
        denom = math.sqrt(DFF)
        q = node_fts @ Wq + bq
        k = node_fts @ Wk + bk
        scores = jnp.einsum('bod,bid->boi', q, k) / denom
        mask = rel_edges == 0
        scores = jnp.where(mask, -1e+18, scores)
        attn = jax.nn.softmax(scores, axis=2)
        attn = jnp.where(mask, 0.0, attn)
        ctx = jnp.einsum('boi,bie->boe', attn, node_fts) @ Wc
        x = node_fts + ctx
        mu = jnp.mean(x, axis=-1, keepdims=True)
        var = jnp.mean(jnp.square(x - mu), axis=-1, keepdims=True)
        out = (x - mu) * jax.lax.rsqrt(var + 1e-05) * gamma + beta
        return out

    def _L2_gnn_ref(feats, adj_mat, fc_w, fc_b, q_w, q_b, k_w, k_b):
        import jax, jax.numpy as jnp
        import numpy as np
        BS, N, H = (8, 1024, 256)
        NEG_INF = -1000000000.0
        LEAKY_SLOPE = 0.01
        feat_proj = jnp.einsum('bnh,oh->bno', feats, fc_w) + fc_b
        q = jnp.einsum('bnh,oh->bno', feat_proj, q_w) + q_b
        k = jnp.einsum('bnh,oh->bno', feat_proj, k_w) + k_b
        logits = q + jnp.swapaxes(k, 2, 1)
        masked = logits + (1.0 - adj_mat) * NEG_INF
        masked = jnp.where(masked >= 0, masked, LEAKY_SLOPE * masked)
        atten = jax.nn.softmax(masked, axis=-1)
        out = jnp.einsum('bnm,bmh->bnh', atten, feat_proj)
        return out + feats

    def _L3_gnn_ref(x, adj, Wq, bq, Wk, bk, Wv, bv, Wo, bo, gamma, beta):
        import jax, jax.numpy as jnp
        import numpy as np
        B, N, D, H = (8, 512, 256, 8)
        DK = D // H
        LN_EPS = 1e-05
        ADJ_MIN = 1e-08

        def _layer_norm(x, gamma, beta):
            mu = jnp.mean(x, axis=-1, keepdims=True)
            var = jnp.mean(jnp.square(x - mu), axis=-1, keepdims=True)
            return (x - mu) * jax.lax.rsqrt(var + LN_EPS) * gamma + beta
        b, n, d = x.shape
        q = (x @ Wq.T + bq).reshape(b, n, H, DK).transpose(0, 2, 1, 3)
        k = (x @ Wk.T + bk).reshape(b, n, H, DK).transpose(0, 2, 1, 3)
        v = (x @ Wv.T + bv).reshape(b, n, H, DK).transpose(0, 2, 1, 3)
        logits = jnp.einsum('bhqd,bhkd->bhqk', q, k) / np.sqrt(DK)
        logits = logits + jnp.log(jnp.clip(adj, ADJ_MIN, None))[:, None, :, :]
        attn = jax.nn.softmax(logits, axis=-1)
        out = jnp.einsum('bhqk,bhkd->bhqd', attn, v)
        out = out.transpose(0, 2, 1, 3).reshape(b, n, d)
        out = out @ Wo.T + bo
        return _layer_norm(x + out, gamma, beta)
    x = _L0_gnn_ref(x, adj, L0_gnn_W_q, L0_gnn_b_q, L0_gnn_W_k, L0_gnn_b_k, L0_gnn_W_v, L0_gnn_b_v, L0_gnn_w_g, L0_gnn_b_g)
    x = _L1_gnn_ref(x, adj, L1_gnn_Wq, L1_gnn_bq, L1_gnn_Wk, L1_gnn_bk, L1_gnn_Wc, L1_gnn_gamma, L1_gnn_beta)
    x = _L2_gnn_ref(x, adj, L2_gnn_fc_w, L2_gnn_fc_b, L2_gnn_q_w, L2_gnn_q_b, L2_gnn_k_w, L2_gnn_k_b)
    x = _L3_gnn_ref(x, adj, L3_gnn_Wq, L3_gnn_bq, L3_gnn_Wk, L3_gnn_bk, L3_gnn_Wv, L3_gnn_bv, L3_gnn_Wo, L3_gnn_bo, L3_gnn_gamma, L3_gnn_beta)
    return x

_drawn_inputs = setup_inputs


def setup_inputs(seed=0):
    import zlib

    import numpy as np

    out = dict(_drawn_inputs(seed))
    spreads = {'L0_gnn_b_q': (0.0, 0.1),
     'L0_gnn_b_k': (0.0, 0.1),
     'L0_gnn_b_v': (0.0, 0.1),
     'L1_gnn_bq': (0.0, 0.1),
     'L1_gnn_bk': (0.0, 0.1),
     'L1_gnn_gamma': (1.0, 0.2),
     'L1_gnn_beta': (0.0, 0.1),
     'L3_gnn_bq': (0.0, 0.1),
     'L3_gnn_bk': (0.0, 0.1),
     'L3_gnn_bv': (0.0, 0.1),
     'L3_gnn_bo': (0.0, 0.1),
     'L3_gnn_gamma': (1.0, 0.2),
     'L3_gnn_beta': (0.0, 0.1)}
    factors = {}
    for name, (base, spread) in spreads.items():
        noise = np.random.default_rng([zlib.crc32(name.encode()), seed]).standard_normal(out[name].shape)
        drawn = base * np.exp(spread * noise) if base else spread * noise
        out[name] = jnp.asarray(drawn.astype(out[name].dtype))
    for name, factor in factors.items():
        out[name] = (out[name] * factor).astype(out[name].dtype)
    return out
```

```python
from contextlib import ExitStack

import concourse.bass as bass
from concourse import mybir

P = 128
D = 256
C = D // P
H = 8
R = 4
HD = D // H
G = 4
U = 2
BANK = 512

LN_EPS = 1e-5
LOG_EPS = 1e-9
ADJ_MIN = 1e-8
MASKED1 = 1e18
MASKED2 = 1e9
LEAK = 0.01

ORDER = [
    "a_xT0", "a_xT1", "a_AT", "b_mask", "a_Q0", "a_K0", "a_Q1", "a_K1", "b_xr0", "b_xr1",
    "a_V0", "a_V1", "a_V2", "a_V3", "a_cols", "b_t0", "b_t1", "a_rows0", "a_rows1",
    "A0_scores", "b_y0", "b_y1", "b_y2", "b_y3", "A0_shift", "b_S",
    "c_AT", "c_Q0", "c_K0", "c_Q1", "c_K1", "C0_scores", "b_soft1",
    "c_V0", "c_V1", "C0_shift", "A0_out", "b_PT", "A1_scores", "b_ctx0", "b_ctx1", "b_ln1",
    "c_xr0", "c_xr1", "A1_shift", "C0_out", "b_xT0", "b_xT1", "C1_scores",
    "b_f0", "b_f1", "b_f2", "b_f3", "b_qk", "C1_shift", "A1_out", "b_kb", "b_soft2", "c_O0",
    "C1_out", "b_P2T", "c_O1", "c_ln3", "b_o0", "b_o1",
]
NO_BANK = ("scores", "shift", "mask", "cols", "soft1", "soft2", "ln1", "ln3", "qk")


def jobs_of(step):
    if step.endswith("_out"):
        return [step[:2] + "_av", step[:2] + "_sum"]
    return [] if step.endswith(NO_BANK) else [step]


class Step:

    def __init__(self, stations, t, before):
        self.stations = stations
        self.order = [s for s in ORDER if s[0].upper() in stations]
        self.quad = {"A": t, "B": t - 1, "C": t - 2}
        jobs = [j for s in self.order for j in jobs_of(s)]
        self.units = [s[:2] for s in self.order if s.endswith("_scores")]
        self.place = {j: (n % 2, n // 2 + 1) for n, j in enumerate(jobs)}
        self.banks = ((len(jobs) + 1) // 2, len(jobs) // 2)
        self.before = before

    def after(self, steps=1):
        return (self.before[0] + steps * self.banks[0], self.before[1] + steps * self.banks[1],
                self.before[2] + steps * len(self.units))

    def turn(self, job):
        bank, n = self.place[job]
        return bank, self.before[bank] + n

    def turns(self, jobs):
        last = {}
        for job in jobs:
            bank, n = self.place[job]
            last[bank] = max(n, last.get(bank, 0))
        return [(bank, self.before[bank] + n) for bank, n in last.items()]

    def unit(self, u):
        return self.before[2] + self.units.index(u)


def gnn_kernel(nc, x, adj, L0_W_q, L0_b_q, L0_W_k, L0_b_k, L0_W_v, L0_b_v, L0_w_g, L0_b_g,
               L1_Wq, L1_bq, L1_Wk, L1_bk, L1_Wc, L1_gamma, L1_beta,
               L2_fc_w, L2_fc_b, L2_q_w, L2_q_b, L2_k_w, L2_k_b,
               L3_Wq, L3_bq, L3_Wk, L3_bk, L3_Wv, L3_bv, L3_Wo, L3_bo, L3_gamma, L3_beta, out):
    fp32, fp32r = mybir.dt.float32, mybir.dt.float32r
    ALU, ACT, AX = mybir.AluOpType, mybir.ActivationFunctionType, mybir.AxisListType
    QUADS = x.shape[0] // G
    SCALE = float(HD) ** -0.5
    SCALE1 = float(D) ** -0.5

    ctx = ExitStack()
    with ctx:
        def sb(name, shape, dt=fp32):
            return ctx.enter_context(nc.sbuf_tensor(name, shape, dt))

        def sem(name):
            return ctx.enter_context(nc.semaphore(name))

        psum = ctx.enter_context(nc.psum_tensor("psum", [P, 8 * BANK], fp32))
        bank = lambda n: psum[:, n * BANK:(n + 1) * BANK]
        scores = [bank(r).rearrange("p (g c j) -> p g c j", g=U, c=C) for r in range(R)]
        turned = [bank(4 + b).rearrange("p (r i) -> p r i", r=R) for b in range(2)]
        general = [bank(6), bank(7)]

        ident = sb("ident", [P, P])
        ident_r = sb("ident_r", [P, P], fp32r)
        ones = sb("ones", [P, HD])
        as_rows = lambda w: w.rearrange("(c p) n -> p c n", p=P)
        as_cols = lambda b: b.rearrange("(c p) -> p c", p=P)
        spread = lambda b: b.rearrange("(a n) -> a n", a=1).broadcast_to([P, b.shape[0]])

        W0q, W0k = sb("W0q", [P, C, D]), sb("W0k", [P, C, D])
        W0v = sb("W0v", [P, C, D + 2])
        b0q, b0k, b0v, b0g = sb("b0q", [P, C]), sb("b0k", [P, C]), sb("b0v", [P, C]), sb("b0g", [P, 1])
        b0q_scaled = sb("b0q_scaled", [P, C])
        W1q, W1k = sb("W1q", [P, C, D]), sb("W1k", [P, C, D])
        W1qT, W1kT = sb("W1qT", [P, C, D]), sb("W1kT", [P, C, D])
        W1qk = sb("W1qk", [P, C, D])
        W1c = sb("W1c", [P, C, D + 1])
        b1q, b1k = sb("b1q", [P, C]), sb("b1k", [P, C])
        u1 = sb("u1", [P, C])
        r1 = sb("r1", [P, 1])
        g1, be1 = sb("g1", [P, C]), sb("be1", [P, C])
        W2 = sb("W2", [P, C, D])
        W2T = sb("W2T", [P, C, D + 2])
        b2, qk2 = sb("b2", [P, C]), sb("qk2", [P, C, 2])
        qkb2, cqk2 = sb("qkb2", [P, 2]), sb("cqk2", [P, 2])
        W3q, W3k, W3v, W3o = (sb(f"W3{n}", [P, C, D]) for n in "qkvo")
        W3qT, W3kT, W3vT, W3oT = (sb(f"W3{n}T", [P, C, D]) for n in "qkvo")
        b3q, b3k, b3v = sb("b3q", [P, C]), sb("b3k", [P, C]), sb("b3v", [P, C])
        b3q_scaled = sb("b3q_scaled", [P, C])
        b3o = sb("b3o", [P, D])
        g3, be3 = sb("g3", [P, D]), sb("be3", [P, D])

        WEIGHTS = [
            (W0q[:, :, :], as_rows(L0_W_q)), (W0k[:, :, :], as_rows(L0_W_k)), (W0v[:, :, 0:D], as_rows(L0_W_v)),
            (W0v[:, :, D], as_cols(L0_w_g[0:D])), (W0v[:, :, D + 1], as_cols(L0_w_g[D:2 * D])),
            (b0q[:, :], as_cols(L0_b_q)), (b0k[:, :], as_cols(L0_b_k)), (b0v[:, :], as_cols(L0_b_v)),
            (b0g[:, :], spread(L0_b_g)),
            (W1q[:, :, :], as_rows(L1_Wq)), (W1k[:, :, :], as_rows(L1_Wk)), (W1c[:, :, 0:D], as_rows(L1_Wc)),
            (b1q[:, :], as_cols(L1_bq)), (b1k[:, :], as_cols(L1_bk)),
            (g1[:, :], as_cols(L1_gamma)), (be1[:, :], as_cols(L1_beta)),
            (W2[:, :, :], as_rows(L2_fc_w)), (b2[:, :], as_cols(L2_fc_b)),
            (qk2[:, :, 0], as_cols(L2_q_w.rearrange("a n -> (a n)"))),
            (qk2[:, :, 1], as_cols(L2_k_w.rearrange("a n -> (a n)"))),
            (qkb2[:, 0:1], spread(L2_q_b)), (qkb2[:, 1:2], spread(L2_k_b)),
            (W3q[:, :, :], as_rows(L3_Wq)), (W3k[:, :, :], as_rows(L3_Wk)), (W3v[:, :, :], as_rows(L3_Wv)),
            (W3o[:, :, :], as_rows(L3_Wo)),
            (b3q[:, :], as_cols(L3_bq)), (b3k[:, :], as_cols(L3_bk)), (b3v[:, :], as_cols(L3_bv)),
            (b3o[:, :], spread(L3_bo)), (g3[:, :], spread(L3_gamma)), (be3[:, :], spread(L3_beta)),
        ]

        x_in = sb("x_in", [P, G, D])
        adjA = sb("adjA", [P, G, P])
        xT = sb("xT", [P, C, G, P])
        wT0 = sb("wT0", [P, G, P])
        qT0, kT0 = sb("qT0", [P, C, G, P]), sb("kT0", [P, C, G, P])
        v0 = sb("v0", [P, G, D + 2])
        ac = sb("ac", [P, G, 2])
        ac_hi = sb("ac_hi", [P, G, 2], fp32r)
        ac_lo = sb("ac_lo", [P, G, 2])
        cols = [sb("cols_i", [P, G, R, HD]), sb("cols_j", [P, G, R, HD])]
        rows = [sb("rows_i", [P, G, P], fp32r), sb("rows_j", [P, G, P], fp32r)]
        x1T = sb("x1T", [P, C, G, P])
        adjB = sb("adjB", [P, G, P])
        edge = sb("edge", [P, G, P])
        far1, far2 = sb("far1", [P, G, P]), sb("far2", [P, G, P])
        x1r = sb("x1r", [P, G, D])
        tT = sb("tT", [P, C, G, P])
        y1 = sb("y1", [P, G, D + 1])
        rr1 = sb("rr1", [P, G])
        s1, e1, p1, p1T = (sb(n, [P, G, P]) for n in ("s1", "e1", "p1", "p1T"))
        nm1, sum1, rs1 = sb("nm1", [P, G]), sb("sum1", [P, G]), sb("rs1", [P, G])
        z1, zn1 = sb("z1", [P, G, D]), sb("zn1", [P, G, D])
        x2T = sb("x2T", [P, C, G, P])
        f2 = sb("f2", [P, G, D + 2])
        qk = sb("qk", [P, G, 2])
        m2, s2, e2, p2, p2T = (sb(n, [P, G, P]) for n in ("m2", "s2", "e2", "p2", "p2T"))
        nm2, sum2, rs2 = sb("nm2", [P, G]), sb("sum2", [P, G]), sb("rs2", [P, G])
        x3T = sb("x3T", [P, C, G, P])
        adjC = sb("adjC", [P, G, P])
        wT3 = sb("wT3", [P, G, P])
        qT3, kT3 = sb("qT3", [P, C, G, P]), sb("kT3", [P, C, G, P])
        v3 = sb("v3", [P, G, D])
        x3r = sb("x3r", [P, G, D])
        oT = sb("oT", [P, C, G, P])
        z3, zn3, o3 = sb("z3", [P, G, D]), sb("zn3", [P, G, D]), sb("o3", [P, G, D])
        negmax = sb("negmax", [P, R, U * C], fp32r)
        expS = [sb(f"expS{n}", [P, R, U, C, P]) for n in range(2)]
        pT = sb("pT", [P, R, U * C, P])
        rinv = sb("rinv", [P, BANK])
        onorm = sb("onorm", [P, U, C, P])
        stats = {n: sb(f"stats{n}", [P, G, 6]) for n in "13"}
        mv = {n: sb(f"mv{n}", [P, G, 2]) for n in "13"}
        lnv, rst0, rst1, rst2, rstd, nmr = ({n: sb(f"{k}{n}", [P, G]) for n in "13"}
                                            for k in ("lnv", "rsta", "rstb", "rstc", "rstd", "nmr"))
        eps_col = sb("eps_col", [P, 1])

        weights_in = sem("weights_in")
        ident_done = sem("ident_done")
        const_done = sem("const_done")
        setup_full = sem("setup_full")
        setup_out = sem("setup_out")
        x_loaded, adjA_loaded, adjB_loaded, adjC_loaded = (sem(n) for n in ("x_in_s", "adjA_s", "adjB_s", "adjC_s"))
        stored = sem("stored")
        full = [sem("full0"), sem("full1")]
        taken = [sem("taken0"), sem("taken1")]
        scored = sem("scored")
        negmaxed = sem("negmaxed")
        shifted = sem("shifted")
        exped = sem("exped")
        t_full = [sem("t_full0"), sem("t_full1")]
        t_taken = [sem("t_taken0"), sem("t_taken1")]
        cols_done = sem("cols_done")
        x1_done = sem("x1_done")
        edge_done, far_done = sem("edge_done"), sem("far_done")
        negmax1, exp1, p1_done = sem("negmax1"), sem("exp1"), sem("p1_done")
        negmax2, exp2, p2_done, qk_done = sem("negmax2"), sem("exp2"), sem("p2_done"), sem("qk_done")
        var_done = {n: sem(f"var_done{n}") for n in "13"}
        rst_done = {n: sem(f"rst_done{n}") for n in "13"}
        norm_done = {n: sem(f"norm_done{n}") for n in "13"}
        zn_done = {n: sem(f"zn_done{n}") for n in "13"}
        chain = {n: sem(f"dve_chain{n}") for n in "ABC"}
        act_chain = {n: sem(f"act_chain{n}") for n in "13"}
        pool_chain = sem("pool_chain")
        passed = sem("passed")
        out_ready = sem("out_ready")

        def need(eng, s, v):
            if not (isinstance(v, int) and v <= 0):
                eng.wait_ge(s, v)

        first = Step("A", 0, (0, 0, 0))
        second = Step("AB", 1, first.after())
        STEADY = QUADS - 2

        def steps(eng, emit):
            emit(first)
            emit(second)
            base = second.after()
            probe = Step("ABC", 2, base)
            with eng.Fori(0, STEADY) as n:
                before = tuple(b + n * (a - b) for b, a in zip(base, probe.after()))
                emit(Step("ABC", n + 2, before))
            late = Step("BC", QUADS, probe.after(STEADY))
            emit(late)
            emit(Step("C", QUADS + 1, late.after()))

        SETUP = ["W1qT0", "W1qT1", "W1kT0", "W1kT1", "W2T0", "W2T1", "W3qT0", "W3qT1", "W3kT0", "W3kT1",
                 "W3vT0", "W3vT1", "W3oT0", "W3oT1", "W1qk0", "W1qk1", "u1", "v1", "r1", "qk2", "cqk2", "b3o"]
        after_setup = len(SETUP)
        LINKS = {"A": 2, "B": 9, "C": 5}
        transposed = {"W1qT": (W1q, W1qT), "W1kT": (W1k, W1kT), "W2T": (W2, W2T), "W3qT": (W3q, W3qT),
                      "W3kT": (W3k, W3kT), "W3vT": (W3v, W3vT), "W3oT": (W3o, W3oT)}

        block = ctx.enter_context(nc.Block())

        @block.sync
        def _(eng):
            graphs = x.rearrange("b p d -> p b d")
            edges = adj.rearrange("b i j -> i b j")
            results = out.rearrange("b p d -> p b d")

            def quad(view, q):
                return view[:, bass.ds(q * G, G), :]

            for dst, src in WEIGHTS:
                eng.dma_start(dst, src, allow_slow_non_contiguous=True).then_inc(weights_in, 16)

            def store(q):
                eng.wait_ge(out_ready, q + 1)
                eng.dma_start(quad(results, q), o3[:, :, :]).then_inc(stored, 16)

            def transfers(step):
                if "A" in step.stations:
                    q = step.quad["A"]
                    need(eng, cols_done, q)
                    eng.dma_start(x_in[:, :, :], quad(graphs, q)).then_inc(x_loaded, 16)
                    eng.dma_start(adjA[:, :, :], quad(edges, q)).then_inc(adjA_loaded, 16)
                if "B" in step.stations:
                    q = step.quad["B"]
                    need(eng, far_done, 2 * q)
                    eng.dma_start(adjB[:, :, :], quad(edges, q)).then_inc(adjB_loaded, 16)
                if "C" in step.stations:
                    q = step.quad["C"]
                    need(eng, var_done["3"], q)
                    eng.dma_start(adjC[:, :, :], quad(edges, q)).then_inc(adjC_loaded, 16)
                    store(q)
            steps(eng, transfers)
            eng.wait_ge(stored, 16 * QUADS)

        @block.gpsimd
        def _(eng):
            eng.memset(ident[:, :], 0.0).then_inc(pool_chain, 1)
            eng.wait_ge(pool_chain, 1)
            eng.affine_select(out=ident[:, :], in_=ident[:, :], compare_op=ALU.not_equal, fill=1.0,
                              base=0, pattern=[[-1, P]], channel_multiplier=1).then_inc(ident_done, 1)

            def work(step):
                if "B" in step.stations:
                    q = step.quad["B"]
                    eng.wait_ge(edge_done, q + 1)
                    eng.sem_inc(passed, 1)
                    eng.tensor_scalar(far1[:, :, :], edge[:, :, :], -1.0, MASKED1, ALU.add, ALU.mult)\
                       .then_inc(far_done, 1)
                    eng.wait_ge(adjB_loaded, 16 * (q + 1))
                    eng.sem_inc(passed, 1)
                    eng.tensor_scalar(far2[:, :, :], adjB[:, :, :], -1.0, MASKED2, ALU.add, ALU.mult)\
                       .then_inc(far_done, 1)
                if "C" in step.stations:
                    q = step.quad["C"]
                    eng.wait_ge(zn_done["3"], q + 1)
                    need(eng, stored, 16 * q)
                    eng.tensor_tensor(o3[:, :, :], zn3[:, :, :], g3[:, :].unsqueeze(1).broadcast_to([P, G, D]),
                                      ALU.mult).then_inc(pool_chain, 1)
                    eng.wait_ge(pool_chain, q + 2)
                    eng.tensor_tensor(o3[:, :, :], o3[:, :, :], be3[:, :].unsqueeze(1).broadcast_to([P, G, D]),
                                      ALU.add).then_inc(out_ready, 1)
            eng.wait_ge(weights_in, 16 * len(WEIGHTS))
            steps(eng, work)

        @block.scalar
        def _(eng):
            eng.wait_ge(setup_out, after_setup)
            act = eng.activation

            def take(step, job, ins_of):
                b, n = step.turn(job)
                eng.wait_ge(full[b], n)
                ins_of(general[b]).then_inc(taken[b], 1)

            def exps(step, u):
                n = step.unit(u)
                e = expS[step.units.index(u) % 2]
                for r in range(R):
                    eng.wait_ge(shifted, R * n + r + 1)
                    act(e[:, r], scores[r], ACT.Exp).then_inc(exped, 1)

            def soft(step, e, s, nm, sums, negmaxed_, exp_):
                q = step.quad["B"]
                eng.wait_ge(negmaxed_, q + 1)
                for g in range(G):
                    act(e[:, g, :], s[:, g, :], ACT.Exp, bias=nm[:, g:g + 1],
                        accum_out=sums[:, g:g + 1]).then_inc(exp_, 1)

            def norm(step, st, k, z, zn):
                q = step.quad[st]
                eng.wait_ge(var_done[k], q + 1)
                act(lnv[k][:, :], mv[k][:, :, 1], ACT.Ln).then_inc(act_chain[k], 1)
                eng.wait_ge(act_chain[k], q + 1)
                act(rst0[k][:, :], lnv[k][:, :], ACT.Exp, scale=-0.5).then_inc(rst_done[k], 1)
                eng.wait_ge(norm_done[k], q + 1)
                if k == "3":
                    need(eng, out_ready, q)
                for g in range(G):
                    last = act(zn[:, g, :], z[:, g, :], ACT.Identity, bias=nmr[k][:, g:g + 1],
                               scale=rstd[k][:, g:g + 1])
                last.then_inc(zn_done[k], 1)

            flat = lambda t, c: t[:, c].rearrange("p g i -> p (g i)")

            def work(step):
                for s in step.order:
                    c = int(s[-1]) if s[-1].isdigit() else 0
                    if s in ("a_xT0", "a_xT1"):
                        need(eng, x1_done, 4 * step.quad["A"])
                        take(step, s, lambda ps: act(flat(xT, c), ps, ACT.Copy))
                    elif s == "a_AT":
                        take(step, s, lambda ps: act(wT0[:, :, :].rearrange("p g i -> p (g i)"), ps, ACT.Identity,
                                                     bias=eps_col[:, 0:1]))
                    elif s in ("a_Q0", "a_Q1"):
                        take(step, s, lambda ps: act(flat(qT0, c), ps, ACT.Identity, bias=b0q_scaled[:, c:c + 1],
                                                     scale=SCALE))
                    elif s in ("a_K0", "a_K1"):
                        take(step, s, lambda ps: act(flat(kT0, c), ps, ACT.Identity, bias=b0k[:, c:c + 1]))
                    elif s[:3] == "a_V":
                        take(step, s, lambda ps: act(v0[:, c, :], ps[:, 0:D + 2], ACT.Copy))
                    elif s in ("b_xr0", "b_xr1"):
                        take(step, s, lambda ps: act(x1r[:, U * c:U * c + U, :].rearrange("p g d -> p (g d)"), ps,
                                                     ACT.Copy))
                    elif s in ("b_t0", "b_t1"):
                        take(step, s, lambda ps: act(flat(tT, c), ps, ACT.Identity, bias=u1[:, c:c + 1]))
                    elif s[:3] == "b_y":
                        take(step, s, lambda ps: act(y1[:, c, :], ps[:, 0:D + 1], ACT.Copy))
                    elif s in ("A0_shift", "A1_shift", "C0_shift", "C1_shift"):
                        exps(step, s[:2])
                    elif s == "b_soft1":
                        soft(step, e1, s1, nm1, sum1, negmax1, exp1)
                    elif s == "b_PT":
                        take(step, s, lambda ps: act(p1T[:, :, :].rearrange("p g i -> p (g i)"), ps, ACT.Copy))
                    elif s == "b_ln1":
                        norm(step, "B", "1", z1, zn1)
                    elif s in ("b_xT0", "b_xT1"):
                        take(step, s, lambda ps: act(flat(x2T, c), ps, ACT.Identity, bias=be1[:, c:c + 1],
                                                     scale=g1[:, c:c + 1]))
                    elif s[:3] == "b_f":
                        take(step, s, lambda ps: act(f2[:, c, :], ps[:, 0:D + 2], ACT.Copy))
                    elif s == "b_soft2":
                        soft(step, e2, s2, nm2, sum2, negmax2, exp2)
                    elif s == "b_P2T":
                        take(step, s, lambda ps: act(p2T[:, :, :].rearrange("p g i -> p (g i)"), ps, ACT.Copy))
                    elif s in ("c_Q0", "c_Q1"):
                        take(step, s, lambda ps: act(flat(qT3, c), ps, ACT.Identity, bias=b3q_scaled[:, c:c + 1],
                                                     scale=SCALE))
                    elif s in ("c_K0", "c_K1"):
                        take(step, s, lambda ps: act(flat(kT3, c), ps, ACT.Identity, bias=b3k[:, c:c + 1]))
                    elif s in ("c_V0", "c_V1"):
                        take(step, s, lambda ps: act(v3[:, U * c:U * c + U, :].rearrange("p g d -> p (g d)"), ps,
                                                     ACT.Copy))
                    elif s == "c_ln3":
                        norm(step, "C", "3", z3, zn3)
            steps(eng, work)

        @block.vector
        def _(eng):
            eng.memset(ones[:, :], 1.0)
            eng.memset(eps_col[:, :], LOG_EPS)
            eng.memset(cols[0][:, :, :, :], 0.0)
            eng.memset(cols[1][:, :, :, :], 0.0).then_inc(const_done, 1)
            eng.wait_ge(const_done, 1)
            eng.memset(cols[0][:, :, :, 0:2], 1.0)
            eng.memset(cols[1][:, :, :, 2:4], 1.0)
            eng.wait_ge(ident_done, 1)
            eng.tensor_copy(ident_r[:, :], ident[:, :]).then_inc(const_done, 1)
            eng.wait_ge(weights_in, 16 * len(WEIGHTS))
            eng.tensor_scalar_mul(b0q_scaled[:, :], b0q[:, :], SCALE)
            eng.tensor_scalar_mul(b3q_scaled[:, :], b3q[:, :], SCALE)
            for n, name in enumerate(SETUP):
                ps, c = bank(n % 2), int(name[-1]) if name[-1].isdigit() else 0
                eng.wait_ge(setup_full, n + 1)
                if name[:-1] in transposed:
                    ins = eng.tensor_copy(transposed[name[:-1]][1][:, c, 0:D], ps[:, 0:D])
                elif name[:-1] == "W1qk":
                    ins = eng.tensor_scalar_mul(W1qk[:, c, :], ps[:, 0:D], SCALE1)
                elif name == "u1":
                    ins = eng.tensor_scalar_mul(u1[:, :], ps[:, 0:C], SCALE1)
                elif name == "v1":
                    ins = eng.tensor_scalar_mul(W1c[:, :, D], ps[:, 0:C], SCALE1)
                elif name == "r1":
                    ins = eng.tensor_scalar_mul(r1[:, :], ps[:, 0:1], SCALE1)
                elif name == "qk2":
                    ins = eng.tensor_copy(W2T[:, :, D:D + 2], ps[:, 0:2 * C].rearrange("p (c n) -> p c n", c=C))
                elif name == "cqk2":
                    ins = eng.tensor_tensor(cqk2[:, :], ps[:, 0:2], qkb2[:, :], ALU.add)
                elif name == "b3o":
                    ins = eng.tensor_tensor(b3o[:, :], ps[:, 0:D], b3o[:, :], ALU.add)
                ins.then_inc(setup_out, 1)

            def work(step):
                links = {st: 0 for st in step.stations}

                def link(st, ins):
                    links[st] += 1
                    ins.then_inc(chain[st], 1)
                    eng.wait_ge(chain[st], LINKS[st] * step.quad[st] + links[st])

                def begin(job):
                    b, n = step.turn(job)
                    eng.wait_ge(full[b], n)
                    return b, n, general[b]

                def maxima(u):
                    n = step.unit(u)
                    eng.wait_ge(scored, n + 1)
                    eng.reduce_max(negmax[:, :, :].rearrange("p r k -> p (r k)"),
                                   psum[:, 0:R * BANK].rearrange("p (k j) -> p k j", j=P),
                                   axis=AX.X, negate=True).then_inc(negmaxed, 1)

                def weigh(u):
                    n = step.unit(u)
                    w = wT0 if u[0] == "A" else wT3
                    for k in range(U * C):
                        g = U * int(u[1]) + k // C
                        eng.wait_ge(t_full[k % 2], 2 * n + k // 2 + 1)
                        eng.tensor_tensor(pT[:, :, k, :], turned[k % 2],
                                          w[:, g, :].unsqueeze(1).broadcast_to([P, R, P]),
                                          ALU.mult).then_inc(t_taken[k % 2], 1)

                def attended(u):
                    h = int(u[1])
                    bs, ns, sums = begin(u + "_sum")
                    eng.reciprocal(rinv[:, :], sums).then_inc(taken[bs], 1)
                    eng.wait_ge(taken[bs], ns)
                    ba, na, values = begin(u + "_av")
                    as_unit = lambda t: t.rearrange("p (g c i) -> p g c i", g=U, c=C)
                    if u[0] == "C":
                        eng.tensor_tensor(oT[:, :, U * h:U * h + U, :].rearrange("p c g i -> p g c i"),
                                          as_unit(values), as_unit(rinv[:, :]), ALU.mult).then_inc(taken[ba], 1)
                        return
                    eng.tensor_tensor(onorm[:, :, :, :], as_unit(values), as_unit(rinv[:, :]),
                                      ALU.mult).then_inc(taken[ba], 1)
                    eng.wait_ge(taken[ba], na)
                    for c in range(C):
                        eng.scalar_tensor_tensor(out=x1T[:, c, U * h:U * h + U, :], in0=onorm[:, :, c, :],
                                                 scalar=b0v[:, c:c + 1], in1=xT[:, c, U * h:U * h + U, :],
                                                 op0=ALU.add, op1=ALU.add).then_inc(x1_done, 1)

                def statistics(st, k, z):
                    q = step.quad[st]
                    for g in range(G):
                        ins = eng.bn_stats(stats[k][:, g, :], z[:, g, :])
                    link(st, ins)
                    eng.sem_inc(passed, 1)
                    for g in range(G):
                        ins = eng.bn_aggr(mv[k][:, g, :], stats[k][:, g, :])
                    link(st, ins)
                    eng.tensor_scalar_add(mv[k][:, :, 1], mv[k][:, :, 1], LN_EPS).then_inc(var_done[k], 1)
                    eng.wait_ge(var_done[k], q + 1)
                    eng.wait_ge(rst_done[k], q + 1)
                    link(st, eng.tensor_tensor(rst1[k][:, :], rst0[k][:, :], rst0[k][:, :], ALU.mult))
                    link(st, eng.scalar_tensor_tensor(out=rst2[k][:, :], in0=rst1[k][:, :], scalar=-0.5,
                                                      in1=mv[k][:, :, 1], op0=ALU.mult, op1=ALU.mult))
                    link(st, eng.scalar_tensor_tensor(out=rstd[k][:, :], in0=rst2[k][:, :], scalar=1.5,
                                                      in1=rst0[k][:, :], op0=ALU.add, op1=ALU.mult))
                    eng.scalar_tensor_tensor(out=nmr[k][:, :], in0=mv[k][:, :, 0], scalar=-1.0,
                                             in1=rstd[k][:, :], op0=ALU.mult, op1=ALU.mult)\
                       .then_inc(norm_done[k], 1)

                for s in step.order:
                    c = int(s[-1]) if s[-1].isdigit() else 0
                    if s == "b_mask":
                        q = step.quad["B"]
                        eng.wait_ge(adjB_loaded, 16 * (q + 1))
                        eng.tensor_scalar(edge[:, :, :], adjB[:, :, :], 0.0, None, ALU.not_equal)\
                           .then_inc(edge_done, 1)
                    elif s == "a_cols":
                        b, n = step.turn("a_V3")
                        eng.wait_ge(taken[b], n)
                        eng.tensor_scalar(ac[:, :, 0], v0[:, :, D], b0g[:, 0:1], None, ALU.add)
                        link("A", eng.tensor_copy(ac[:, :, 1], v0[:, :, D + 1]))
                        link("A", eng.tensor_copy(ac_hi[:, :, :], ac[:, :, :]))
                        hi = ac_hi[:, :, :].bitcast(fp32)
                        tiles = lambda t, n: t[:, :, n:n + 1].broadcast_to([P, G, R])
                        eng.tensor_copy(cols[0][:, :, :, 2], tiles(hi, 0))
                        eng.tensor_tensor(cols[0][:, :, :, 3], tiles(ac, 0), tiles(hi, 0), ALU.subtract)
                        eng.tensor_copy(cols[1][:, :, :, 0], tiles(hi, 1))
                        eng.tensor_tensor(cols[1][:, :, :, 1], tiles(ac, 1), tiles(hi, 1), ALU.subtract)\
                           .then_inc(cols_done, 1)
                    elif s in ("a_rows0", "a_rows1"):
                        b, n, ps = begin(s)
                        eng.tensor_copy(rows[c][:, :, :].rearrange("p g i -> p (g i)"), ps)\
                           .then_inc(taken[b], 1)
                    elif s in ("A0_scores", "A1_scores", "C0_scores", "C1_scores"):
                        maxima(s[:2])
                    elif s in ("A0_out", "A1_out", "C0_out", "C1_out"):
                        weigh(s[:2])
                        attended(s[:2])
                    elif s == "b_S":
                        b, n = step.turn("b_y3")
                        eng.wait_ge(taken[b], n)
                        link("B", eng.tensor_scalar(rr1[:, :], y1[:, :, D], r1[:, 0:1], None, ALU.add))
                        eng.wait_ge(far_done, 2 * step.quad["B"] + 2)
                        b, n, ps = begin(s)
                        for g in range(G):
                            ins = eng.scalar_tensor_tensor(out=s1[:, g, :], in0=ps[:, g * P:(g + 1) * P],
                                                           scalar=rr1[:, g:g + 1], in1=far1[:, g, :],
                                                           op0=ALU.add, op1=ALU.add)
                        ins.then_inc(taken[b], 1)
                        eng.wait_ge(taken[b], n)
                        eng.reduce_max(nm1[:, :], s1[:, :, :], axis=AX.X, negate=True).then_inc(negmax1, 1)
                    elif s == "b_soft1":
                        eng.wait_ge(exp1, G * (step.quad["B"] + 1))
                        link("B", eng.reciprocal(rs1[:, :], sum1[:, :]))
                        for g in range(G):
                            ins = eng.scalar_tensor_tensor(out=p1[:, g, :], in0=e1[:, g, :], scalar=rs1[:, g:g + 1],
                                                           in1=edge[:, g, :], op0=ALU.mult, op1=ALU.mult)
                        ins.then_inc(p1_done, 1)
                    elif s in ("b_ctx0", "b_ctx1"):
                        b, n, ps = begin(s)
                        if c == 0:
                            need(eng, zn_done["1"], step.quad["B"])
                            bx, nx = step.turn("b_xr1")
                            eng.wait_ge(taken[bx], nx)
                        eng.tensor_tensor(z1[:, U * c:U * c + U, :].rearrange("p g d -> p (g d)"), ps,
                                          x1r[:, U * c:U * c + U, :].rearrange("p g d -> p (g d)"), ALU.add)\
                           .then_inc(taken[b], 1)
                    elif s == "b_ln1":
                        for b, n in step.turns(("b_ctx0", "b_ctx1")):
                            eng.wait_ge(taken[b], n)
                        statistics("B", "1", z1)
                    elif s == "b_qk":
                        b, n = step.turn("b_f3")
                        eng.wait_ge(taken[b], n)
                        eng.tensor_tensor(qk[:, :, :], f2[:, :, D:D + 2],
                                          cqk2[:, :].unsqueeze(1).broadcast_to([P, G, 2]), ALU.add)\
                           .then_inc(qk_done, 1)
                    elif s == "b_kb":
                        b, n, ps = begin(s)
                        eng.wait_ge(qk_done, step.quad["B"] + 1)
                        for g in range(G):
                            ins = eng.scalar_tensor_tensor(out=m2[:, g, :], in0=ps[:, g * P:(g + 1) * P],
                                                           scalar=qk[:, g, 0:1], in1=far2[:, g, :],
                                                           op0=ALU.add, op1=ALU.add)
                        ins.then_inc(taken[b], 1)
                        eng.wait_ge(taken[b], n)
                        link("B", eng.scalar_tensor_tensor(out=s2[:, :, :], in0=m2[:, :, :], scalar=LEAK,
                                                           in1=m2[:, :, :], op0=ALU.mult, op1=ALU.max))
                        eng.reduce_max(nm2[:, :], s2[:, :, :], axis=AX.X, negate=True).then_inc(negmax2, 1)
                    elif s == "b_soft2":
                        eng.wait_ge(exp2, G * (step.quad["B"] + 1))
                        link("B", eng.reciprocal(rs2[:, :], sum2[:, :]))
                        eng.tensor_tensor(p2[:, :, :], e2[:, :, :], rs2[:, :].unsqueeze(2).broadcast_to([P, G, P]),
                                          ALU.mult).then_inc(p2_done, 1)
                    elif s in ("b_o0", "b_o1"):
                        b, n, ps = begin(s)
                        eng.scalar_tensor_tensor(out=x3T[:, c].rearrange("p g i -> p (g i)"), in0=ps,
                                                 scalar=b2[:, c:c + 1],
                                                 in1=x2T[:, c].rearrange("p g i -> p (g i)"),
                                                 op0=ALU.add, op1=ALU.add).then_inc(taken[b], 1)
                    elif s == "c_AT":
                        b, n, ps = begin(s)
                        eng.tensor_scalar_max(wT3[:, :, :].rearrange("p g i -> p (g i)"), ps, ADJ_MIN)\
                           .then_inc(taken[b], 1)
                    elif s in ("c_xr0", "c_xr1"):
                        b, n, ps = begin(s)
                        eng.tensor_tensor(x3r[:, U * c:U * c + U, :], ps.rearrange("p (g d) -> p g d", g=U),
                                          b3o[:, :].unsqueeze(1).broadcast_to([P, U, D]), ALU.add)\
                           .then_inc(taken[b], 1)
                    elif s in ("c_O0", "c_O1"):
                        b, n, ps = begin(s)
                        if c == 0:
                            need(eng, zn_done["3"], step.quad["C"])
                            bx, nx = step.turn("c_xr1")
                            eng.wait_ge(taken[bx], nx)
                        eng.tensor_tensor(z3[:, U * c:U * c + U, :].rearrange("p g d -> p (g d)"), ps,
                                          x3r[:, U * c:U * c + U, :].rearrange("p g d -> p (g d)"), ALU.add)\
                           .then_inc(taken[b], 1)
                    elif s == "c_ln3":
                        for b, n in step.turns(("c_O0", "c_O1")):
                            eng.wait_ge(taken[b], n)
                        statistics("C", "3", z3)
                assert all(links[st] == LINKS[st] for st in links)
            steps(eng, work)

        @block.tensor
        def _(eng):
            mm = eng.matmul
            eng.wait_ge(weights_in, 16 * len(WEIGHTS))
            eng.wait_ge(ident_done, 1)
            eng.wait_ge(const_done, 2)
            for n, name in enumerate(SETUP):
                ps, c = bank(n % 2), int(name[-1]) if name[-1].isdigit() else 0
                need(eng, setup_out, n - 1)
                if name in ("W1qk0", "u1", "b3o"):
                    eng.wait_ge(setup_out, n)
                for k in range(C):
                    part = slice(k * P, (k + 1) * P)
                    two = dict(start=k == 0, stop=k == C - 1)
                    if name[:-1] in transposed:
                        last = eng.transpose(ps[:, part], transposed[name[:-1]][0][:, k, c * P:(c + 1) * P], ident[:, :])
                    elif name[:-1] == "W1qk":
                        last = mm(ps[:, 0:D], W1qT[:, k, c * P:(c + 1) * P], W1kT[:, k, :], **two)
                    elif name == "r1":
                        last = mm(ps[:, 0:1], b1q[:, k:k + 1].broadcast_to([P, P]), b1k[:, k:k + 1], **two)
                    elif name == "cqk2":
                        last = mm(ps[:, 0:2], b2[:, k:k + 1].broadcast_to([P, P]), qk2[:, k, :], **two)
                    elif name == "b3o":
                        last = mm(ps[:, 0:D], b3v[:, k:k + 1].broadcast_to([P, P]), W3oT[:, k, :], **two)
                if name in ("u1", "v1", "qk2"):
                    w, b, width = {"u1": (W1kT, b1q, 1), "v1": (W1qT, b1k, 1), "qk2": (W2, qk2, 2)}[name]
                    for c in range(C):
                        for k in range(C):
                            rhs = b[:, k, :] if width == 2 else b[:, k:k + 1]
                            last = mm(ps[:, c * width:(c + 1) * width], w[:, k, c * P:(c + 1) * P], rhs,
                                      start=k == 0, stop=k == C - 1)
                last.then_inc(setup_full, 1)
            eng.wait_ge(setup_out, after_setup)

            def work(step):
                def begin(job, *inputs):
                    b, n = step.turn(job)
                    need(eng, taken[b], n - 1)
                    for other, m in step.turns(inputs):
                        if other != b:
                            eng.wait_ge(taken[other], m)
                    return b, general[b]

                def ready(*jobs):
                    for b, n in step.turns(jobs):
                        eng.wait_ge(taken[b], n)

                def turn_in(job, parts):
                    b, ps = begin(job)
                    for n, part in enumerate(parts):
                        last = eng.transpose(ps[:, n * P:(n + 1) * P], part, ident[:, :])
                    last.then_inc(full[b], 1)

                def project_T(job, w, c, src, *inputs):
                    b, ps = begin(job, *inputs)
                    for k in range(C):
                        last = mm(ps, w[:, k, c * P:(c + 1) * P], src[:, k].rearrange("p g i -> p (g i)"),
                                  start=k == 0, stop=k == C - 1)
                    last.then_inc(full[b], 1)

                def project(job, src, graphs, w, width, *inputs):
                    b, ps = begin(job, *inputs)
                    for n, g in enumerate(graphs):
                        for k in range(C):
                            last = mm(ps[:, n * width:(n + 1) * width], src[:, k, g, :], w[:, k, 0:width],
                                      start=k == 0, stop=k == C - 1)
                    last.then_inc(full[b], 1)

                def score(u):
                    n, h = step.unit(u), int(u[1])
                    qT, kT = (qT0, kT0) if u[0] == "A" else (qT3, kT3)
                    need(eng, exped, R * n)
                    if u[0] == "A":
                        for g in range(U):
                            for r in range(R):
                                lanes = slice(HD * r, HD * r + 4)
                                mm(scores[r][:, g], rows[0][lanes, U * h + g, :],
                                   rows[1][lanes, U * h + g, :].unsqueeze(1).broadcast_to([4, C, P]),
                                   start=g == 0, stop=False, skip_group_check=True)
                    for g in range(U):
                        for c in range(C):
                            for r in range(R):
                                lanes = slice(HD * r, HD * (r + 1))
                                last = mm(scores[r][:, g, c, :], qT[lanes, c, U * h + g, :],
                                          kT[lanes, c, U * h + g, :],
                                          start=u[0] == "C" and g == 0 and c == 0, stop=False,
                                          skip_group_check=True)
                    last.then_inc(scored, 1)

                def shift(u):
                    eng.wait_ge(negmaxed, step.unit(u) + 1)
                    for r in range(R):
                        mm(bank(r), ident_r[:, :], negmax[:, r, :].unsqueeze(2).broadcast_to([P, U * C, P]),
                           start=False, stop=True, skip_group_check=True).then_inc(shifted, 1)

                def attend(u):
                    n, h = step.unit(u), int(u[1])
                    e, v = expS[step.units.index(u) % 2], (v0 if u[0] == "A" else v3)
                    eng.wait_ge(exped, R * (n + 1))

                    def turn(k):
                        need(eng, t_taken[k % 2], 2 * n + k // 2)
                        for r in range(R):
                            last = eng.transpose(turned[k % 2][:, r, :], e[:, r, k // C, k % C, :], ident[:, :])
                        last.then_inc(t_full[k % 2], 1)

                    def values(k):
                        eng.wait_ge(t_taken[k % 2], 2 * n + k // 2 + 1)
                        for r in range(R):
                            col = (k % C) * P + HD * r
                            last = mm(av[HD * r:HD * (r + 1), k * P:(k + 1) * P],
                                      v[:, U * h + k // C, col:col + HD], pT[:, r, k, :], start=True, stop=True)
                        return last

                    turn(0)
                    turn(1)
                    ba, av = begin(u + "_av")
                    values(0)
                    turn(2)
                    values(1)
                    turn(3)
                    values(2)
                    values(3).then_inc(full[ba], 1)
                    bs, sums = begin(u + "_sum")
                    for r in range(R):
                        last = mm(sums[HD * r:HD * (r + 1), :], ones[:, :],
                                  pT[:, r, :, :].rearrange("p k i -> p (k i)"), start=True, stop=True)
                    last.then_inc(full[bs], 1)

                qA, qB, qC = (step.quad[st] for st in "ABC")
                for s in step.order:
                    c = int(s[-1]) if s[-1].isdigit() else 0
                    chunk = slice(c * P, (c + 1) * P)
                    if s[:3] == "a_x":
                        if c == 0:
                            eng.wait_ge(x_loaded, 16 * (qA + 1))
                        turn_in(s, [x_in[:, g, chunk] for g in range(G)])
                    elif s == "a_AT":
                        eng.wait_ge(adjA_loaded, 16 * (qA + 1))
                        turn_in(s, [adjA[:, g, :] for g in range(G)])
                    elif s in ("a_Q0", "a_Q1", "a_K0", "a_K1"):
                        project_T(s, W0q if s[2] == "Q" else W0k, c, xT, "a_xT0", "a_xT1")
                    elif s[:3] == "a_V":
                        project(s, xT, [c], W0v, D + 2)
                    elif s in ("a_rows0", "a_rows1"):
                        if c == 0:
                            eng.wait_ge(cols_done, qA + 1)
                        turn_in(s, [cols[c][:, g].rearrange("p r n -> p (r n)") for g in range(G)])
                    elif s in ("A0_scores", "A1_scores"):
                        if s[1] == "0":
                            ready("a_Q0", "a_Q1", "a_K0", "a_K1", "a_rows0", "a_rows1")
                        score(s[:2])
                    elif s in ("C0_scores", "C1_scores"):
                        if s[1] == "0":
                            ready("c_Q0", "c_Q1", "c_K0", "c_K1")
                        score(s[:2])
                    elif s.endswith("_shift"):
                        shift(s[:2])
                    elif s in ("A0_out", "A1_out", "C0_out", "C1_out"):
                        attend(s[:2])
                    elif s in ("b_xr0", "b_xr1"):
                        if c == 0:
                            eng.wait_ge(x1_done, 2 * C * (qB + 1))
                        turn_in(s, [x1T[:, k, U * c + g, :] for g in range(U) for k in range(C)])
                    elif s in ("b_t0", "b_t1"):
                        project_T(s, W1qk, c, x1T)
                    elif s[:3] == "b_y":
                        project(s, x1T, [c], W1c, D + 1)
                    elif s == "b_S":
                        b, ps = begin(s, "b_t0", "b_t1")
                        for g in range(G):
                            for k in range(C):
                                last = mm(ps[:, g * P:(g + 1) * P], tT[:, k, g, :], x1T[:, k, g, :],
                                          start=k == 0, stop=k == C - 1)
                        last.then_inc(full[b], 1)
                    elif s == "b_PT":
                        eng.wait_ge(p1_done, qB + 1)
                        turn_in(s, [p1[:, g, :] for g in range(G)])
                    elif s in ("b_ctx0", "b_ctx1"):
                        b, ps = begin(s, "b_PT", f"b_y{U * c + 1}")
                        for g in range(U):
                            last = mm(ps[:, g * D:(g + 1) * D], p1T[:, U * c + g, :], y1[:, U * c + g, 0:D],
                                      start=True, stop=True)
                        last.then_inc(full[b], 1)
                    elif s in ("b_xT0", "b_xT1"):
                        eng.wait_ge(zn_done["1"], qB + 1)
                        turn_in(s, [zn1[:, g, chunk] for g in range(G)])
                    elif s[:3] == "b_f":
                        project(s, x2T, [c], W2T, D + 2, "b_xT0", "b_xT1")
                    elif s == "b_kb":
                        eng.wait_ge(qk_done, qB + 1)
                        turn_in(s, [qk[:, g, 1:2].broadcast_to([P, P]) for g in range(G)])
                    elif s == "b_P2T":
                        eng.wait_ge(p2_done, qB + 1)
                        turn_in(s, [p2[:, g, :] for g in range(G)])
                    elif s in ("b_o0", "b_o1"):
                        b, ps = begin(s, "b_P2T")
                        for g in range(G):
                            last = mm(ps[:, g * P:(g + 1) * P], f2[:, g, chunk], p2T[:, g, :], start=True, stop=True)
                        last.then_inc(full[b], 1)
                    elif s == "c_AT":
                        eng.wait_ge(adjC_loaded, 16 * (qC + 1))
                        turn_in(s, [adjC[:, g, :] for g in range(G)])
                    elif s in ("c_Q0", "c_Q1", "c_K0", "c_K1"):
                        project_T(s, W3qT if s[2] == "Q" else W3kT, c, x3T)
                    elif s in ("c_V0", "c_V1"):
                        project(s, x3T, [U * c, U * c + 1], W3vT, D)
                    elif s in ("c_xr0", "c_xr1"):
                        turn_in(s, [x3T[:, k, U * c + g, :] for g in range(U) for k in range(C)])
                    elif s in ("c_O0", "c_O1"):
                        project(s, oT, [U * c, U * c + 1], W3oT, D, f"C{c}_av")
            steps(eng, work)


_INS = ['x', 'adj', 'L0_gnn_W_q', 'L0_gnn_b_q', 'L0_gnn_W_k', 'L0_gnn_b_k', 'L0_gnn_W_v', 'L0_gnn_b_v',
        'L0_gnn_w_g', 'L0_gnn_b_g', 'L1_gnn_Wq', 'L1_gnn_bq', 'L1_gnn_Wk', 'L1_gnn_bk', 'L1_gnn_Wc',
        'L1_gnn_gamma', 'L1_gnn_beta', 'L2_gnn_fc_w', 'L2_gnn_fc_b', 'L2_gnn_q_w', 'L2_gnn_q_b',
        'L2_gnn_k_w', 'L2_gnn_k_b', 'L3_gnn_Wq', 'L3_gnn_bq', 'L3_gnn_Wk', 'L3_gnn_bk', 'L3_gnn_Wv',
        'L3_gnn_bv', 'L3_gnn_Wo', 'L3_gnn_bo', 'L3_gnn_gamma', 'L3_gnn_beta']


def kernel(**inputs):
    import numpy as _np
    import concourse.bacc as _bacc
    from concourse import mybir as _mybir
    from concourse.bass_utils import run_bass_kernel_spmd as _run

    nc = _bacc.Bacc("TRN2", target_bir_lowering=False, num_devices=1)
    arrays, args = {}, []
    for name in _INS:
        a = _np.ascontiguousarray(inputs[name])
        a = a.reshape(a.shape or (1,))
        arrays[f"in_{name}_dram"] = a
        args.append(nc.dram_tensor(f"in_{name}_dram", a.shape, _mybir.dt.from_np(a.dtype), kind="ExternalInput").ap())
    shape = _np.asarray(inputs["x"]).shape
    out = nc.dram_tensor("out_0_dram", shape, _mybir.dt.float32, kind="ExternalOutput").ap()
    gnn_kernel(nc, *args, out)
    r = _run(nc, [arrays], core_ids=[0])
    return r.results[0]["out_0_dram"]
```

```python
from contextlib import ExitStack

import concourse.bass as bass
from concourse import mybir

P = 128
D = 256
C = D // P
H = 8
R = 4
HD = D // H
G = 4
U = 2
BANK = 512

LN_EPS = 1e-5
LOG_EPS = 1e-9
ADJ_MIN = 1e-8
MASKED1 = 1e18
MASKED2 = 1e9
LEAK = 0.01

TILES = G * C


def tile_slots(station, work):
    order = []
    for n in range(TILES):
        order += [f"{station}_score{n}"]
        if n % C == 0 and n:
            order += [f"{station}_out{n // C - 1}"]
        order += [*work[2 * n].split(), f"{station}_shift{n}", *work[2 * n + 1].split(), f"{station}_turn{n}"]
    return order


ORDER = (
    tile_slots("C", [
        "a_xT0 a_xT1 b_mask b_xr0 b_xr1", "a_Q0",
        "b_t0", "b_t1",
        "b_y0 b_y1", "b_y2 b_y3",
        "b_S", "a_K0",
        "b_exp1 a_V0 a_V1", "b_p1 a_V2",
        "a_AT a_V3", "a_cols b_PT a_Q1",
        "b_ctx0 b_ctx1", "b_st1 a_K1",
        "b_rs1 a_rows0 a_rows1", "b_nw1 b_zn1",
    ])
    + tile_slots("A", [
        "C_out3", "b_xT0 b_xT1",
        "b_f0 b_f1", "b_f2 b_f3 b_qk",
        "b_kb", "c_O0",
        "b_exp2 c_O1", "b_p2 c_AT c_st3",
        "b_P2T c_rs3", "b_o0 b_o1 c_nw3",
        "c_Q0 c_zn3", "c_K0",
        "c_Q1", "c_K1",
        "c_V0", "c_V1",
    ])
    + ["c_xr0", "c_xr1", "A_out3"]
)
NO_BANK = {"score", "shift", "turn", "cols", "mask", "exp", "p", "qk", "st", "rs", "nw", "zn"}
BANKS = 4
STATION = {"c_Q": "B", "c_K": "B", "c_V": "B", "c_A": "B", "c_x": "B"}


class Step:

    def __init__(self, stations, t, before):
        self.stations = stations
        self.order = [s for s in ORDER if STATION.get(s[:3], s[0].upper()) in stations]
        self.quad = {"A": t, "B": t - 1, "C": t - 2}
        jobs = [s for s in self.order if s[2:].rstrip("0123456789") not in NO_BANK]
        self.tiled = [s[0] for s in self.order if s.endswith("_score0")]
        self.place = {j: (n % BANKS, n // BANKS + 1) for n, j in enumerate(jobs)}
        self.jobs = [len(range(b, len(jobs), BANKS)) for b in range(BANKS)]
        self.before = before

    def after(self, steps=1):
        jobs, tiles = self.before
        return ([n + steps * m for n, m in zip(jobs, self.jobs)], tiles + steps * TILES * len(self.tiled))

    def turn(self, job):
        bank, n = self.place[job]
        return bank, self.before[0][bank] + n

    def turns(self, jobs):
        last = {}
        for job in jobs:
            bank, n = self.place[job]
            last[bank] = max(n, last.get(bank, 0))
        return [(bank, self.before[0][bank] + n) for bank, n in last.items()]

    def tile(self, station, n):
        return self.before[1] + TILES * self.tiled.index(station) + n


def gnn_kernel(nc, x, adj, L0_W_q, L0_b_q, L0_W_k, L0_b_k, L0_W_v, L0_b_v, L0_w_g, L0_b_g,
               L1_Wq, L1_bq, L1_Wk, L1_bk, L1_Wc, L1_gamma, L1_beta,
               L2_fc_w, L2_fc_b, L2_q_w, L2_q_b, L2_k_w, L2_k_b,
               L3_Wq, L3_bq, L3_Wk, L3_bk, L3_Wv, L3_bv, L3_Wo, L3_bo, L3_gamma, L3_beta, out):
    fp32, fp32r = mybir.dt.float32, mybir.dt.float32r
    ALU, ACT, AX = mybir.AluOpType, mybir.ActivationFunctionType, mybir.AxisListType
    QUADS = x.shape[0] // G
    SCALE = float(HD) ** -0.5
    SCALE1 = float(D) ** -0.5

    ctx = ExitStack()
    with ctx:
        def sb(name, shape, dt=fp32):
            return ctx.enter_context(nc.sbuf_tensor(name, shape, dt))

        def sem(name):
            return ctx.enter_context(nc.semaphore(name))

        psum = ctx.enter_context(nc.psum_tensor("psum", [P, 8 * BANK], fp32))
        bank = lambda n: psum[:, n * BANK:(n + 1) * BANK]
        scores = [bank(n).rearrange("p (r j) -> p r j", r=R) for n in range(2)]
        turned = [bank(2 + n).rearrange("p (r i) -> p r i", r=R) for n in range(2)]
        general = [bank(4 + n) for n in range(BANKS)]

        ident = sb("ident", [P, P])
        ident_r = sb("ident_r", [P, P], fp32r)
        ones = sb("ones", [P, HD])
        as_rows = lambda w: w.rearrange("(c p) n -> p c n", p=P)
        as_cols = lambda b: b.rearrange("(c p) -> p c", p=P)
        spread = lambda b: b.rearrange("(a n) -> a n", a=1).broadcast_to([P, b.shape[0]])

        z1, zn1, z3, zn3, o3 = (sb(n, [P, G, D]) for n in ("z1", "zn1", "z3", "zn3", "o3"))
        raw = lambda t, n: t[:, C * n:C * (n + 1), :]

        W0q, W0k = sb("W0q", [P, C, D]), sb("W0k", [P, C, D])
        W0v = sb("W0v", [P, C, D + 2])
        b0q, b0k, b0v, b0g = sb("b0q", [P, C]), sb("b0k", [P, C]), sb("b0v", [P, C]), sb("b0g", [P, 1])
        b0q_scaled = sb("b0q_scaled", [P, C])
        W1q, W1k, W1qT, W1kT = raw(z3, 0), raw(z3, 1), raw(zn1, 0), raw(zn1, 1)
        W1qk = sb("W1qk", [P, C, D])
        W1c = sb("W1c", [P, C, D + 1])
        b1q, b1k = sb("b1q", [P, C]), sb("b1k", [P, C])
        u1 = sb("u1", [P, C])
        r1 = sb("r1", [P, 1])
        g1, be1 = sb("g1", [P, C]), sb("be1", [P, C])
        W2 = raw(zn3, 0)
        W2T = sb("W2T", [P, C, D + 2])
        b2, qk2 = sb("b2", [P, C]), sb("qk2", [P, C, 2])
        qkb2, cqk2 = sb("qkb2", [P, 2]), sb("cqk2", [P, 2])
        W3q, W3k, W3v, W3o = raw(zn3, 1), raw(o3, 0), raw(o3, 1), raw(z1, 0)
        W3qT, W3kT, W3vT, W3oT = (sb(f"W3{n}T", [P, C, D]) for n in "qkvo")
        b3q, b3k, b3v = sb("b3q", [P, C]), sb("b3k", [P, C]), sb("b3v", [P, C])
        b3q_scaled = sb("b3q_scaled", [P, C])
        b3o = sb("b3o", [P, D])
        g3, be3 = sb("g3", [P, D]), sb("be3", [P, D])

        WEIGHTS = [
            (W0q[:, :, :], as_rows(L0_W_q)), (W0k[:, :, :], as_rows(L0_W_k)), (W0v[:, :, 0:D], as_rows(L0_W_v)),
            (W0v[:, :, D], as_cols(L0_w_g[0:D])), (W0v[:, :, D + 1], as_cols(L0_w_g[D:2 * D])),
            (b0q[:, :], as_cols(L0_b_q)), (b0k[:, :], as_cols(L0_b_k)), (b0v[:, :], as_cols(L0_b_v)),
            (b0g[:, :], spread(L0_b_g)),
            (W1q[:, :, :], as_rows(L1_Wq)), (W1k[:, :, :], as_rows(L1_Wk)), (W1c[:, :, 0:D], as_rows(L1_Wc)),
            (b1q[:, :], as_cols(L1_bq)), (b1k[:, :], as_cols(L1_bk)),
            (g1[:, :], as_cols(L1_gamma)), (be1[:, :], as_cols(L1_beta)),
            (W2[:, :, :], as_rows(L2_fc_w)), (b2[:, :], as_cols(L2_fc_b)),
            (qk2[:, :, 0], as_cols(L2_q_w.rearrange("a n -> (a n)"))),
            (qk2[:, :, 1], as_cols(L2_k_w.rearrange("a n -> (a n)"))),
            (qkb2[:, 0:1], spread(L2_q_b)), (qkb2[:, 1:2], spread(L2_k_b)),
            (W3q[:, :, :], as_rows(L3_Wq)), (W3k[:, :, :], as_rows(L3_Wk)), (W3v[:, :, :], as_rows(L3_Wv)),
            (W3o[:, :, :], as_rows(L3_Wo)),
            (b3q[:, :], as_cols(L3_bq)), (b3k[:, :], as_cols(L3_bk)), (b3v[:, :], as_cols(L3_bv)),
            (b3o[:, :], spread(L3_bo)), (g3[:, :], spread(L3_gamma)), (be3[:, :], spread(L3_beta)),
        ]

        x_in = sb("x_in", [P, G, D])
        adjA = sb("adjA", [P, G, P])
        xT = sb("xT", [P, C, G, P])
        wT0 = sb("wT0", [P, G, P])
        qT0 = sb("qT0", [P, C, G, P])
        kD0 = sb("kD0", [P, C, G, R, P])
        v0 = sb("v0", [P, G, D + 2])
        ac = sb("ac", [P, G, 2])
        ac_hi = sb("ac_hi", [P, G, 2], fp32r)
        ac_lo = sb("ac_lo", [P, G, 2])
        cols = [sb("cols_i", [P, G, 4]), sb("cols_j", [P, G, 4])]
        rows = [sb("rows_i", [4, G, P], fp32r), sb("rows_j", [4, G, P], fp32r)]
        x1T = sb("x1T", [P, C, G, P])
        adjB = sb("adjB", [P, G, P])
        edge = sb("edge", [P, G, P])
        far1, far2 = sb("far1", [P, G, P]), sb("far2", [P, G, P])
        x1r = sb("x1r", [P, G, D])
        tT = sb("tT", [P, C, G, P])
        y1 = sb("y1", [P, G, D + 1])
        rr1 = sb("rr1", [P, G])
        s1, e1, p1, p1T = (sb(n, [P, G, P]) for n in ("s1", "e1", "p1", "p1T"))
        nm1, sum1, rs1 = sb("nm1", [P, G]), sb("sum1", [P, G]), sb("rs1", [P, G])
        x2T = sb("x2T", [P, C, G, P])
        f2 = sb("f2", [P, G, D + 2])
        qk = sb("qk", [P, G, 2])
        m2, s2, e2, p2, p2T = (sb(n, [P, G, P]) for n in ("m2", "s2", "e2", "p2", "p2T"))
        nm2, sum2, rs2 = sb("nm2", [P, G]), sb("sum2", [P, G]), sb("rs2", [P, G])
        x3T = sb("x3T", [P, C, G, P])
        adjC = sb("adjC", [P, G, P])
        wT3 = sb("wT3", [P, G, P])
        qT3, kD3 = sb("qT3", [P, C, G, P]), sb("kD3", [P, C, G, R, P])
        v3 = sb("v3", [P, G, D])
        x3r = sb("x3r", [P, G, D])
        oT = sb("oT", [P, C, G, P])
        negmax = sb("negmax", [P, 2, R], fp32r)
        expS = sb("expS", [P, 2, R, P])
        pT = sb("pT", [P, R, 2 * C, P])
        rinv = sb("rinv", [P, C, P])
        onorm = sb("onorm", [P, C, P])
        stats = {n: sb(f"stats{n}", [P, G, 6]) for n in "13"}
        mv = {n: sb(f"mv{n}", [P, G, 2]) for n in "13"}
        lnv, rst0, rst1, rst2, rstd, nmr = ({n: sb(f"{k}{n}", [P, G]) for n in "13"}
                                            for k in ("lnv", "rsta", "rstb", "rstc", "rstd", "nmr"))
        eps_col = sb("eps_col", [P, 1])

        weights_in = sem("weights_in")
        ident_done = sem("ident_done")
        const_done = sem("const_done")
        setup_full = sem("setup_full")
        setup_out = sem("setup_out")
        x_loaded, adjA_loaded, adjB_loaded, adjC_loaded = (sem(n) for n in ("x_in_s", "adjA_s", "adjB_s", "adjC_s"))
        stored = sem("stored")
        full = [sem(f"full{b}") for b in range(BANKS)]
        taken = [sem(f"taken{b}") for b in range(BANKS)]
        scored = sem("scored")
        negmaxed = sem("negmaxed")
        shifted = sem("shifted")
        exped = sem("exped")
        t_full = sem("t_full")
        t_taken = sem("t_taken")
        cols_done = sem("cols_done")
        x1_done = sem("x1_done")
        edge_done, far_done = sem("edge_done"), sem("far_done")
        x3r_done = sem("x3r_done")
        proj3_done = sem("proj3_done")
        wT3_done = sem("wT3_done")
        negmax1, exp1, p1_done = sem("negmax1"), sem("exp1"), sem("p1_done")
        negmax2, exp2, p2_done, qk_done = sem("negmax2"), sem("exp2"), sem("p2_done"), sem("qk_done")
        var_done = {n: sem(f"var_done{n}") for n in "13"}
        rst_done = {n: sem(f"rst_done{n}") for n in "13"}
        norm_done = {n: sem(f"norm_done{n}") for n in "13"}
        zn_done = {n: sem(f"zn_done{n}") for n in "13"}
        chain = {n: sem(f"dve_chain{n}") for n in "ABC"}
        act_chain = {n: sem(f"act_chain{n}") for n in "13"}
        pool_chain = sem("pool_chain")
        passed = sem("passed")
        out_ready = sem("out_ready")

        def need(eng, s, v):
            if not (isinstance(v, int) and v <= 0):
                eng.wait_ge(s, v)

        first = Step("A", 0, ([0] * BANKS, 0))
        second = Step("AB", 1, first.after())
        STEADY = QUADS - 2

        def steps(eng, emit):
            emit(first)
            emit(second)
            base = second.after()
            probe = Step("ABC", 2, base)
            with eng.Fori(0, STEADY) as n:
                jobs = [b + n * m for b, m in zip(base[0], probe.jobs)]
                emit(Step("ABC", n + 2, (jobs, base[1] + n * TILES * len(probe.tiled))))
            late = Step("BC", QUADS, probe.after(STEADY))
            emit(late)
            emit(Step("C", QUADS + 1, late.after()))

        SETUP = ["W1qT0", "W1qT1", "W1kT0", "W1kT1", "W2T0", "W2T1", "W3qT0", "W3qT1", "W3kT0", "W3kT1",
                 "W3vT0", "W3vT1", "W3oT0", "W3oT1", "W1qk0", "W1qk1", "u1", "v1", "r1", "qk2", "cqk2", "b3o"]
        after_setup = len(SETUP)
        LINKS = {"A": 2 + G, "B": 9, "C": 5 + G}
        transposed = {"W1qT": (W1q, W1qT), "W1kT": (W1k, W1kT), "W2T": (W2, W2T), "W3qT": (W3q, W3qT),
                      "W3kT": (W3k, W3kT), "W3vT": (W3v, W3vT), "W3oT": (W3o, W3oT)}

        block = ctx.enter_context(nc.Block())

        @block.sync
        def _(eng):
            graphs = x.rearrange("b p d -> p b d")
            edges = adj.rearrange("b i j -> i b j")

            def quad(view, q):
                return view[:, bass.ds(q * G, G), :]

            for dst, src in WEIGHTS:
                eng.dma_start(dst, src, allow_slow_non_contiguous=True).then_inc(weights_in, 16)

            def transfers(step):
                if "A" in step.stations:
                    q = step.quad["A"]
                    need(eng, cols_done, q)
                    eng.dma_start(x_in[:, :, :], quad(graphs, q)).then_inc(x_loaded, 16)
                    eng.dma_start(adjA[:, :, :], quad(edges, q)).then_inc(adjA_loaded, 16)
                if "B" in step.stations:
                    q = step.quad["B"]
                    need(eng, far_done, 2 * q)
                    eng.dma_start(adjB[:, :, :], quad(edges, q)).then_inc(adjB_loaded, 16)
                    need(eng, wT3_done, q)
                    eng.dma_start(adjC[:, :, :], quad(edges, q)).then_inc(adjC_loaded, 16)
            steps(eng, transfers)

        @block.gpsimd
        def _(eng):
            eng.memset(ident[:, :], 0.0).then_inc(pool_chain, 1)
            eng.wait_ge(pool_chain, 1)
            eng.affine_select(out=ident[:, :], in_=ident[:, :], compare_op=ALU.not_equal, fill=1.0,
                              base=0, pattern=[[-1, P]], channel_multiplier=1).then_inc(ident_done, 1)

            def work(step):
                if "B" in step.stations:
                    q = step.quad["B"]
                    eng.wait_ge(edge_done, q + 1)
                    eng.sem_inc(passed, 1)
                    eng.tensor_scalar(far1[:, :, :], edge[:, :, :], -1.0, MASKED1, ALU.add, ALU.mult)\
                       .then_inc(far_done, 1)
                    eng.wait_ge(adjB_loaded, 16 * (q + 1))
                    eng.sem_inc(passed, 1)
                    eng.tensor_scalar(far2[:, :, :], adjB[:, :, :], -1.0, MASKED2, ALU.add, ALU.mult)\
                       .then_inc(far_done, 1)
                if "C" in step.stations:
                    q = step.quad["C"]
                    eng.wait_ge(zn_done["3"], q + 1)
                    need(eng, stored, 16 * q)
                    eng.tensor_tensor(o3[:, :, :], zn3[:, :, :], g3[:, :].unsqueeze(1).broadcast_to([P, G, D]),
                                      ALU.mult).then_inc(pool_chain, 1)
                    eng.wait_ge(pool_chain, q + 2)
                    eng.tensor_tensor(o3[:, :, :], o3[:, :, :], be3[:, :].unsqueeze(1).broadcast_to([P, G, D]),
                                      ALU.add).then_inc(out_ready, 1)
                    eng.wait_ge(out_ready, q + 1)
                    eng.sem_inc(passed, 1)
                    eng.dma_start(results[:, bass.ds(q * G, G), :], o3[:, :, :]).then_inc(stored, 16)
            results = out.rearrange("b p d -> p b d")
            eng.wait_ge(weights_in, 16 * len(WEIGHTS))
            steps(eng, work)
            eng.wait_ge(stored, 16 * QUADS)

        @block.scalar
        def _(eng):
            eng.preload_act_table_set("natural_log_exp_and_others")
            eng.wait_ge(setup_out, after_setup)
            act = eng.activation

            def take(step, job, ins_of):
                b, n = step.turn(job)
                eng.wait_ge(full[b], n)
                ins_of(general[b]).then_inc(taken[b], 1)

            def blocks(k_blocks, c, ps, bias):
                for r in range(R):
                    lanes = slice(HD * r, HD * (r + 1))
                    last = act(k_blocks[lanes, c, :, r, :], ps[lanes, :].rearrange("p (g j) -> p g j", g=G),
                               ACT.Identity, bias=bias[lanes, c:c + 1])
                return last

            def soft(step, e, s, nm, sums, negmaxed_, exp_):
                q = step.quad["B"]
                eng.wait_ge(negmaxed_, q + 1)
                for g in range(G):
                    act(e[:, g, :], s[:, g, :], ACT.Exp, bias=nm[:, g:g + 1],
                        accum_out=sums[:, g:g + 1]).then_inc(exp_, 1)

            def estimate(step, st, k):
                q = step.quad[st]
                eng.wait_ge(var_done[k], q + 1)
                act(lnv[k][:, :], mv[k][:, :, 1], ACT.Ln).then_inc(act_chain[k], 1)
                eng.wait_ge(act_chain[k], q + 1)
                act(rst0[k][:, :], lnv[k][:, :], ACT.Exp, scale=-0.5).then_inc(rst_done[k], 1)

            def normalise(step, st, k, z, zn):
                q = step.quad[st]
                eng.wait_ge(norm_done[k], q + 1)
                if k == "3":
                    need(eng, out_ready, q)
                for g in range(G):
                    last = act(zn[:, g, :], z[:, g, :], ACT.Identity, bias=nmr[k][:, g:g + 1],
                               scale=rstd[k][:, g:g + 1])
                last.then_inc(zn_done[k], 1)

            flat = lambda t, c: t[:, c].rearrange("p g i -> p (g i)")

            def work(step):
                for s in step.order:
                    c = int(s[-1]) if s[-1].isdigit() else 0
                    if s in ("a_xT0", "a_xT1"):
                        need(eng, x1_done, C * G * step.quad["A"])
                        take(step, s, lambda ps: act(flat(xT, c), ps, ACT.Copy))
                    elif s == "a_AT":
                        take(step, s, lambda ps: act(wT0[:, :, :].rearrange("p g i -> p (g i)"), ps, ACT.Identity,
                                                     bias=eps_col[:, 0:1]))
                    elif s in ("a_Q0", "a_Q1"):
                        take(step, s, lambda ps: act(flat(qT0, c), ps, ACT.Identity, bias=b0q_scaled[:, c:c + 1],
                                                     scale=SCALE))
                    elif s in ("a_K0", "a_K1"):
                        take(step, s, lambda ps: blocks(kD0, c, ps, b0k))
                    elif s[:3] == "a_V":
                        take(step, s, lambda ps: act(v0[:, c, :], ps[:, 0:D + 2], ACT.Copy))
                    elif s in ("b_xr0", "b_xr1"):
                        take(step, s, lambda ps: act(x1r[:, U * c:U * c + U, :].rearrange("p g d -> p (g d)"), ps,
                                                     ACT.Copy))
                    elif s in ("b_t0", "b_t1"):
                        take(step, s, lambda ps: act(flat(tT, c), ps, ACT.Identity, bias=u1[:, c:c + 1]))
                    elif s[:3] == "b_y":
                        take(step, s, lambda ps: act(y1[:, c, :], ps[:, 0:D + 1], ACT.Copy))
                    elif s[2:7] == "shift":
                        n = step.tile(s[0], c)
                        eng.wait_ge(shifted, n + 1)
                        act(expS[:, c % 2], scores[c % 2], ACT.Exp).then_inc(exped, 1)
                    elif s == "b_exp1":
                        soft(step, e1, s1, nm1, sum1, negmax1, exp1)
                    elif s == "b_PT":
                        take(step, s, lambda ps: act(p1T[:, :, :].rearrange("p g i -> p (g i)"), ps, ACT.Copy))
                    elif s in ("b_rs1", "c_rs3"):
                        estimate(step, s[0].upper(), s[-1])
                    elif s == "b_zn1":
                        normalise(step, "B", "1", z1, zn1)
                    elif s in ("b_xT0", "b_xT1"):
                        take(step, s, lambda ps: act(flat(x2T, c), ps, ACT.Identity, bias=be1[:, c:c + 1],
                                                     scale=g1[:, c:c + 1]))
                    elif s[:3] == "b_f":
                        take(step, s, lambda ps: act(f2[:, c, :], ps[:, 0:D + 2], ACT.Copy))
                    elif s == "b_exp2":
                        soft(step, e2, s2, nm2, sum2, negmax2, exp2)
                    elif s == "b_P2T":
                        take(step, s, lambda ps: act(p2T[:, :, :].rearrange("p g i -> p (g i)"), ps, ACT.Copy))
                    elif s in ("c_Q0", "c_Q1"):
                        take(step, s, lambda ps: act(flat(qT3, c), ps, ACT.Identity, bias=b3q_scaled[:, c:c + 1],
                                                     scale=SCALE))
                    elif s in ("c_K0", "c_K1"):
                        take(step, s, lambda ps: blocks(kD3, c, ps, b3k))
                    elif s in ("c_V0", "c_V1"):
                        take(step, s, lambda ps: act(v3[:, U * c:U * c + U, :].rearrange("p g d -> p (g d)"), ps,
                                                     ACT.Copy))
                        if c == 1:
                            for b, n in step.turns(("c_Q0", "c_Q1", "c_K0", "c_K1", "c_V0", "c_V1")):
                                eng.wait_ge(taken[b], n)
                            eng.sem_inc(proj3_done, 1)
                    elif s == "c_zn3":
                        normalise(step, "C", "3", z3, zn3)
            steps(eng, work)

        @block.vector
        def _(eng):
            eng.memset(ones[:, :], 1.0)
            eng.memset(eps_col[:, :], LOG_EPS)
            eng.memset(cols[0][:, :, :], 1.0)
            eng.memset(cols[1][:, :, :], 1.0)
            eng.memset(kD0[:, :, :, :, :], 0.0)
            eng.memset(kD3[:, :, :, :, :], 0.0).then_inc(const_done, 1)
            eng.wait_ge(ident_done, 1)
            eng.tensor_copy(ident_r[:, :], ident[:, :]).then_inc(const_done, 1)
            eng.wait_ge(weights_in, 16 * len(WEIGHTS))
            eng.tensor_scalar_mul(b0q_scaled[:, :], b0q[:, :], SCALE)
            eng.tensor_scalar_mul(b3q_scaled[:, :], b3q[:, :], SCALE)
            for n, name in enumerate(SETUP):
                ps, c = bank(n % 2), int(name[-1]) if name[-1].isdigit() else 0
                eng.wait_ge(setup_full, n + 1)
                if name[:-1] in transposed:
                    ins = eng.tensor_copy(transposed[name[:-1]][1][:, c, 0:D], ps[:, 0:D])
                elif name[:-1] == "W1qk":
                    ins = eng.tensor_scalar_mul(W1qk[:, c, :], ps[:, 0:D], SCALE1)
                elif name == "u1":
                    ins = eng.tensor_scalar_mul(u1[:, :], ps[:, 0:C], SCALE1)
                elif name == "v1":
                    ins = eng.tensor_scalar_mul(W1c[:, :, D], ps[:, 0:C], SCALE1)
                elif name == "r1":
                    ins = eng.tensor_scalar_mul(r1[:, :], ps[:, 0:1], SCALE1)
                elif name == "qk2":
                    ins = eng.tensor_copy(W2T[:, :, D:D + 2], ps[:, 0:2 * C].rearrange("p (c n) -> p c n", c=C))
                elif name == "cqk2":
                    ins = eng.tensor_tensor(cqk2[:, :], ps[:, 0:2], qkb2[:, :], ALU.add)
                elif name == "b3o":
                    ins = eng.tensor_tensor(b3o[:, :], ps[:, 0:D], b3o[:, :], ALU.add)
                ins.then_inc(setup_out, 1)

            def work(step):
                links = {st: 0 for st in step.stations}

                def link(st, ins):
                    links[st] += 1
                    ins.then_inc(chain[st], 1)
                    eng.wait_ge(chain[st], LINKS[st] * step.quad[st] + links[st])

                def begin(job):
                    b, n = step.turn(job)
                    eng.wait_ge(full[b], n)
                    return b, n, general[b]

                def ready(*jobs):
                    for b, n in step.turns(jobs):
                        eng.wait_ge(taken[b], n)

                def maxima(st, n):
                    eng.wait_ge(scored, step.tile(st, n) + 1)
                    eng.reduce_max(negmax[:, n % 2, :], scores[n % 2], axis=AX.X, negate=True)\
                       .then_inc(negmaxed, 1)

                def weigh(st, n):
                    w = wT0 if st == "A" else wT3
                    if n == 0 and st == "A":
                        ready("a_AT")
                    eng.wait_ge(t_full, step.tile(st, n) + 1)
                    eng.tensor_tensor(pT[:, :, n % (2 * C), :], turned[n % 2],
                                      w[:, n // C, :].unsqueeze(1).broadcast_to([P, R, P]),
                                      ALU.mult).then_inc(t_taken, 1)

                def attended(s, st, g):
                    b, n, ps = begin(s)
                    both = ps.rearrange("p (t c i) -> p t c i", t=2, c=C)
                    link(st, eng.reciprocal(rinv[:, :, :], both[:, 1]))
                    if st == "C":
                        eng.tensor_tensor(oT[:, :, g, :], both[:, 0], rinv[:, :, :], ALU.mult)\
                           .then_inc(taken[b], 1)
                        return
                    eng.tensor_tensor(onorm[:, :, :], both[:, 0], rinv[:, :, :], ALU.mult).then_inc(taken[b], 1)
                    eng.wait_ge(taken[b], n)
                    for c in range(C):
                        eng.scalar_tensor_tensor(out=x1T[:, c, g, :], in0=onorm[:, c, :],
                                                 scalar=b0v[:, c:c + 1], in1=xT[:, c, g, :],
                                                 op0=ALU.add, op1=ALU.add).then_inc(x1_done, 1)

                def statistics(st, k, z):
                    for g in range(G):
                        ins = eng.bn_stats(stats[k][:, g, :], z[:, g, :])
                    link(st, ins)
                    eng.sem_inc(passed, 1)
                    for g in range(G):
                        ins = eng.bn_aggr(mv[k][:, g, :], stats[k][:, g, :])
                    link(st, ins)
                    eng.tensor_scalar_add(mv[k][:, :, 1], mv[k][:, :, 1], LN_EPS).then_inc(var_done[k], 1)

                def refine(st, k):
                    q = step.quad[st]
                    eng.wait_ge(var_done[k], q + 1)
                    eng.wait_ge(rst_done[k], q + 1)
                    link(st, eng.tensor_tensor(rst1[k][:, :], rst0[k][:, :], rst0[k][:, :], ALU.mult))
                    link(st, eng.scalar_tensor_tensor(out=rst2[k][:, :], in0=rst1[k][:, :], scalar=-0.5,
                                                      in1=mv[k][:, :, 1], op0=ALU.mult, op1=ALU.mult))
                    link(st, eng.scalar_tensor_tensor(out=rstd[k][:, :], in0=rst2[k][:, :], scalar=1.5,
                                                      in1=rst0[k][:, :], op0=ALU.add, op1=ALU.mult))
                    eng.scalar_tensor_tensor(out=nmr[k][:, :], in0=mv[k][:, :, 0], scalar=-1.0,
                                             in1=rstd[k][:, :], op0=ALU.mult, op1=ALU.mult)\
                       .then_inc(norm_done[k], 1)

                for s in step.order:
                    c = int(s[-1]) if s[-1].isdigit() else 0
                    if s == "b_mask":
                        q = step.quad["B"]
                        eng.wait_ge(adjB_loaded, 16 * (q + 1))
                        eng.tensor_scalar(edge[:, :, :], adjB[:, :, :], 0.0, None, ALU.not_equal)\
                           .then_inc(edge_done, 1)
                    elif s == "a_cols":
                        b, n = step.turn("a_V3")
                        eng.wait_ge(taken[b], n)
                        eng.tensor_scalar(ac[:, :, 0], v0[:, :, D], b0g[:, 0:1], None, ALU.add)
                        link("A", eng.tensor_copy(ac[:, :, 1], v0[:, :, D + 1]))
                        link("A", eng.tensor_copy(ac_hi[:, :, :], ac[:, :, :]))
                        hi = ac_hi[:, :, :].bitcast(fp32)
                        eng.tensor_copy(cols[0][:, :, 2], hi[:, :, 0])
                        eng.tensor_tensor(cols[0][:, :, 3], ac[:, :, 0], hi[:, :, 0], ALU.subtract)
                        eng.tensor_copy(cols[1][:, :, 0], hi[:, :, 1])
                        eng.tensor_tensor(cols[1][:, :, 1], ac[:, :, 1], hi[:, :, 1], ALU.subtract)\
                           .then_inc(cols_done, 1)
                    elif s in ("a_rows0", "a_rows1"):
                        b, n, ps = begin(s)
                        eng.tensor_copy(rows[c][:, :, :].rearrange("p g i -> p (g i)"), ps[0:4, :])\
                           .then_inc(taken[b], 1)
                    elif s[2:7] == "score":
                        maxima(s[0], c)
                    elif s[2:6] == "turn":
                        weigh(s[0], c)
                    elif s[1:5] == "_out":
                        attended(s, s[0], c)
                    elif s == "b_S":
                        b, n = step.turn("b_y3")
                        eng.wait_ge(taken[b], n)
                        link("B", eng.tensor_scalar(rr1[:, :], y1[:, :, D], r1[:, 0:1], None, ALU.add))
                        eng.wait_ge(far_done, 2 * step.quad["B"] + 2)
                        b, n, ps = begin(s)
                        for g in range(G):
                            ins = eng.scalar_tensor_tensor(out=s1[:, g, :], in0=ps[:, g * P:(g + 1) * P],
                                                           scalar=rr1[:, g:g + 1], in1=far1[:, g, :],
                                                           op0=ALU.add, op1=ALU.add)
                        ins.then_inc(taken[b], 1)
                        eng.wait_ge(taken[b], n)
                        eng.reduce_max(nm1[:, :], s1[:, :, :], axis=AX.X, negate=True).then_inc(negmax1, 1)
                    elif s == "b_p1":
                        eng.wait_ge(exp1, G * (step.quad["B"] + 1))
                        link("B", eng.reciprocal(rs1[:, :], sum1[:, :]))
                        for g in range(G):
                            ins = eng.scalar_tensor_tensor(out=p1[:, g, :], in0=e1[:, g, :], scalar=rs1[:, g:g + 1],
                                                           in1=edge[:, g, :], op0=ALU.mult, op1=ALU.mult)
                        ins.then_inc(p1_done, 1)
                    elif s in ("b_ctx0", "b_ctx1"):
                        b, n, ps = begin(s)
                        if c == 0:
                            need(eng, zn_done["1"], step.quad["B"])
                            ready("b_xr0", "b_xr1")
                        eng.tensor_tensor(z1[:, U * c:U * c + U, :].rearrange("p g d -> p (g d)"), ps,
                                          x1r[:, U * c:U * c + U, :].rearrange("p g d -> p (g d)"), ALU.add)\
                           .then_inc(taken[b], 1)
                    elif s == "b_st1":
                        for b, n in step.turns(("b_ctx0", "b_ctx1")):
                            eng.wait_ge(taken[b], n)
                        statistics("B", "1", z1)
                    elif s in ("b_nw1", "c_nw3"):
                        refine(s[0].upper(), s[-1])
                    elif s == "b_qk":
                        b, n = step.turn("b_f3")
                        eng.wait_ge(taken[b], n)
                        eng.tensor_tensor(qk[:, :, :], f2[:, :, D:D + 2],
                                          cqk2[:, :].unsqueeze(1).broadcast_to([P, G, 2]), ALU.add)\
                           .then_inc(qk_done, 1)
                    elif s == "b_kb":
                        b, n, ps = begin(s)
                        eng.wait_ge(qk_done, step.quad["B"] + 1)
                        for g in range(G):
                            ins = eng.scalar_tensor_tensor(out=m2[:, g, :], in0=ps[:, g * P:(g + 1) * P],
                                                           scalar=qk[:, g, 0:1], in1=far2[:, g, :],
                                                           op0=ALU.add, op1=ALU.add)
                        ins.then_inc(taken[b], 1)
                        eng.wait_ge(taken[b], n)
                        link("B", eng.scalar_tensor_tensor(out=s2[:, :, :], in0=m2[:, :, :], scalar=LEAK,
                                                           in1=m2[:, :, :], op0=ALU.mult, op1=ALU.max))
                        eng.reduce_max(nm2[:, :], s2[:, :, :], axis=AX.X, negate=True).then_inc(negmax2, 1)
                    elif s == "b_p2":
                        eng.wait_ge(exp2, G * (step.quad["B"] + 1))
                        link("B", eng.reciprocal(rs2[:, :], sum2[:, :]))
                        eng.tensor_tensor(p2[:, :, :], e2[:, :, :], rs2[:, :].unsqueeze(2).broadcast_to([P, G, P]),
                                          ALU.mult).then_inc(p2_done, 1)
                    elif s in ("b_o0", "b_o1"):
                        b, n, ps = begin(s)
                        eng.scalar_tensor_tensor(out=x3T[:, c].rearrange("p g i -> p (g i)"), in0=ps,
                                                 scalar=b2[:, c:c + 1],
                                                 in1=x2T[:, c].rearrange("p g i -> p (g i)"),
                                                 op0=ALU.add, op1=ALU.add).then_inc(taken[b], 1)
                    elif s == "c_AT":
                        b, n, ps = begin(s)
                        eng.tensor_scalar_max(wT3[:, :, :].rearrange("p g i -> p (g i)"), ps, ADJ_MIN)\
                           .then_inc(taken[b], 1)
                        ready(s)
                        eng.sem_inc(wT3_done, 1)
                    elif s in ("c_xr0", "c_xr1"):
                        b, n, ps = begin(s)
                        eng.tensor_tensor(x3r[:, U * c:U * c + U, :], ps.rearrange("p (g d) -> p g d", g=U),
                                          b3o[:, :].unsqueeze(1).broadcast_to([P, U, D]), ALU.add)\
                           .then_inc(taken[b], 1)
                        if c == 1:
                            ready("c_xr0", "c_xr1")
                            eng.sem_inc(x3r_done, 1)
                    elif s in ("c_O0", "c_O1"):
                        b, n, ps = begin(s)
                        if c == 0:
                            need(eng, zn_done["3"], step.quad["C"])
                            eng.wait_ge(x3r_done, step.quad["C"] + 1)
                        eng.tensor_tensor(z3[:, U * c:U * c + U, :].rearrange("p g d -> p (g d)"), ps,
                                          x3r[:, U * c:U * c + U, :].rearrange("p g d -> p (g d)"), ALU.add)\
                           .then_inc(taken[b], 1)
                    elif s == "c_st3":
                        for b, n in step.turns(("c_O0", "c_O1")):
                            eng.wait_ge(taken[b], n)
                        statistics("C", "3", z3)
                assert all(links[st] == LINKS[st] for st in links)
            steps(eng, work)

        @block.tensor
        def _(eng):
            mm = eng.matmul
            eng.wait_ge(weights_in, 16 * len(WEIGHTS))
            eng.wait_ge(ident_done, 1)
            eng.wait_ge(const_done, 2)
            for n, name in enumerate(SETUP):
                ps, c = bank(n % 2), int(name[-1]) if name[-1].isdigit() else 0
                need(eng, setup_out, n - 1)
                if name in ("W1qk0", "u1", "b3o"):
                    eng.wait_ge(setup_out, n)
                for k in range(C):
                    part = slice(k * P, (k + 1) * P)
                    two = dict(start=k == 0, stop=k == C - 1)
                    if name[:-1] in transposed:
                        last = eng.transpose(ps[:, part], transposed[name[:-1]][0][:, k, c * P:(c + 1) * P], ident[:, :])
                    elif name[:-1] == "W1qk":
                        last = mm(ps[:, 0:D], W1qT[:, k, c * P:(c + 1) * P], W1kT[:, k, :], **two)
                    elif name == "r1":
                        last = mm(ps[:, 0:1], b1q[:, k:k + 1].broadcast_to([P, P]), b1k[:, k:k + 1], **two)
                    elif name == "cqk2":
                        last = mm(ps[:, 0:2], b2[:, k:k + 1].broadcast_to([P, P]), qk2[:, k, :], **two)
                    elif name == "b3o":
                        last = mm(ps[:, 0:D], b3v[:, k:k + 1].broadcast_to([P, P]), W3oT[:, k, :], **two)
                if name in ("u1", "v1", "qk2"):
                    w, b, width = {"u1": (W1kT, b1q, 1), "v1": (W1qT, b1k, 1), "qk2": (W2, qk2, 2)}[name]
                    for c in range(C):
                        for k in range(C):
                            rhs = b[:, k, :] if width == 2 else b[:, k:k + 1]
                            last = mm(ps[:, c * width:(c + 1) * width], w[:, k, c * P:(c + 1) * P], rhs,
                                      start=k == 0, stop=k == C - 1)
                last.then_inc(setup_full, 1)
            eng.wait_ge(setup_out, after_setup)

            def work(step):
                def begin(job, *inputs):
                    b, n = step.turn(job)
                    need(eng, taken[b], n - 1)
                    for other, m in step.turns(inputs):
                        if other != b:
                            eng.wait_ge(taken[other], m)
                    return b, general[b]

                def ready(*jobs):
                    for b, n in step.turns(jobs):
                        eng.wait_ge(taken[b], n)

                def turn_in(job, parts):
                    b, ps = begin(job)
                    for n, part in enumerate(parts):
                        last = eng.transpose(ps[0:part.shape[-1], n * P:(n + 1) * P], part, ident[:, :])
                    last.then_inc(full[b], 1)

                def project_T(job, w, c, src, *inputs):
                    b, ps = begin(job, *inputs)
                    for k in range(C):
                        last = mm(ps, w[:, k, c * P:(c + 1) * P], src[:, k].rearrange("p g i -> p (g i)"),
                                  start=k == 0, stop=k == C - 1)
                    last.then_inc(full[b], 1)

                def project(job, src, graphs, w, width, *inputs):
                    b, ps = begin(job, *inputs)
                    for n, g in enumerate(graphs):
                        for k in range(C):
                            last = mm(ps[:, n * width:(n + 1) * width], src[:, k, g, :], w[:, k, 0:width],
                                      start=k == 0, stop=k == C - 1)
                    last.then_inc(full[b], 1)

                def score(st, n):
                    g, c, out = n // C, n % C, bank(n % 2)
                    qT, kD = (qT0, kD0) if st == "A" else (qT3, kD3)
                    need(eng, exped, step.tile(st, n) - 1)
                    if st == "A":
                        mm(out, rows[0][:, g, :], rows[1][:, g, :].unsqueeze(1).broadcast_to([4, R, P]),
                           start=True, stop=False, skip_group_check=True)
                    mm(out, qT[:, c, g, :], kD[:, c, g].rearrange("p r j -> p (r j)"),
                       start=st == "C", stop=False, skip_group_check=True).then_inc(scored, 1)

                def shift(st, n):
                    eng.wait_ge(negmaxed, step.tile(st, n) + 1)
                    mm(bank(n % 2), ident_r[:, :], negmax[:, n % 2, :].unsqueeze(2).broadcast_to([P, R, P]),
                       start=False, stop=True, skip_group_check=True).then_inc(shifted, 1)

                def turn(st, n):
                    eng.wait_ge(exped, step.tile(st, n) + 1)
                    need(eng, t_taken, step.tile(st, n) - 1)
                    for r in range(R):
                        last = eng.transpose(turned[n % 2][:, r, :], expS[:, n % 2, r, :], ident[:, :])
                    last.then_inc(t_full, 1)

                def attend(s, st, g):
                    v = v0 if st == "A" else v3
                    b, ps = begin(s)
                    eng.wait_ge(t_taken, step.tile(st, C * g) + C)
                    first = C * (g % 2)
                    for c in range(C):
                        for r in range(R):
                            col = c * P + HD * r
                            mm(ps[HD * r:HD * (r + 1), c * P:(c + 1) * P], v[:, g, col:col + HD],
                               pT[:, r, first + c, :], start=True, stop=True)
                    for r in range(R):
                        last = mm(ps[HD * r:HD * (r + 1), C * P:2 * C * P], ones[:, :],
                                  pT[:, r, first:first + C, :].rearrange("p c i -> p (c i)"),
                                  start=True, stop=True)
                    last.then_inc(full[b], 1)

                qA, qB, qC = (step.quad[st] for st in "ABC")
                for s in step.order:
                    c = int(s[-1]) if s[-1].isdigit() else 0
                    chunk = slice(c * P, (c + 1) * P)
                    if s[:3] == "a_x":
                        if c == 0:
                            eng.wait_ge(x_loaded, 16 * (qA + 1))
                        turn_in(s, [x_in[:, g, chunk] for g in range(G)])
                    elif s == "a_AT":
                        eng.wait_ge(adjA_loaded, 16 * (qA + 1))
                        turn_in(s, [adjA[:, g, :] for g in range(G)])
                    elif s in ("a_Q0", "a_Q1", "a_K0", "a_K1"):
                        project_T(s, W0q if s[2] == "Q" else W0k, c, xT, "a_xT0", "a_xT1")
                    elif s[:3] == "a_V":
                        project(s, xT, [c], W0v, D + 2)
                    elif s in ("a_rows0", "a_rows1"):
                        if c == 0:
                            eng.wait_ge(cols_done, qA + 1)
                        turn_in(s, [cols[c][:, g, :] for g in range(G)])
                    elif s[2:7] == "score":
                        if s == "A_score0":
                            ready("a_Q0", "a_K0", "a_rows0", "a_rows1")
                        elif s == "A_score1":
                            ready("a_Q1", "a_K1")
                        elif s == "C_score0":
                            eng.wait_ge(proj3_done, qC + 1)
                        score(s[0], c)
                    elif s[2:7] == "shift":
                        shift(s[0], c)
                    elif s[2:6] == "turn":
                        turn(s[0], c)
                    elif s[1:5] == "_out":
                        if s == "A_out0":
                            ready("a_V0", "a_V1", "a_V2", "a_V3")
                        attend(s, s[0], c)
                    elif s in ("b_xr0", "b_xr1"):
                        if c == 0:
                            eng.wait_ge(x1_done, C * G * (qB + 1))
                        turn_in(s, [x1T[:, k, U * c + g, :] for g in range(U) for k in range(C)])
                    elif s in ("b_t0", "b_t1"):
                        project_T(s, W1qk, c, x1T)
                    elif s[:3] == "b_y":
                        project(s, x1T, [c], W1c, D + 1)
                    elif s == "b_S":
                        b, ps = begin(s, "b_t0", "b_t1")
                        for g in range(G):
                            for k in range(C):
                                last = mm(ps[:, g * P:(g + 1) * P], tT[:, k, g, :], x1T[:, k, g, :],
                                          start=k == 0, stop=k == C - 1)
                        last.then_inc(full[b], 1)
                    elif s == "b_PT":
                        eng.wait_ge(p1_done, qB + 1)
                        turn_in(s, [p1[:, g, :] for g in range(G)])
                    elif s in ("b_ctx0", "b_ctx1"):
                        b, ps = begin(s, "b_PT", f"b_y{U * c + 1}")
                        for g in range(U):
                            last = mm(ps[:, g * D:(g + 1) * D], p1T[:, U * c + g, :], y1[:, U * c + g, 0:D],
                                      start=True, stop=True)
                        last.then_inc(full[b], 1)
                    elif s in ("b_xT0", "b_xT1"):
                        eng.wait_ge(zn_done["1"], qB + 1)
                        turn_in(s, [zn1[:, g, chunk] for g in range(G)])
                    elif s[:3] == "b_f":
                        project(s, x2T, [c], W2T, D + 2, "b_xT0", "b_xT1")
                    elif s == "b_kb":
                        eng.wait_ge(qk_done, qB + 1)
                        turn_in(s, [qk[:, g, 1:2].broadcast_to([P, P]) for g in range(G)])
                    elif s == "b_P2T":
                        eng.wait_ge(p2_done, qB + 1)
                        turn_in(s, [p2[:, g, :] for g in range(G)])
                    elif s in ("b_o0", "b_o1"):
                        b, ps = begin(s, "b_P2T")
                        for g in range(G):
                            last = mm(ps[:, g * P:(g + 1) * P], f2[:, g, chunk], p2T[:, g, :], start=True, stop=True)
                        last.then_inc(full[b], 1)
                    elif s == "c_AT":
                        eng.wait_ge(adjC_loaded, 16 * (qB + 1))
                        turn_in(s, [adjC[:, g, :] for g in range(G)])
                    elif s in ("c_Q0", "c_Q1", "c_K0", "c_K1"):
                        project_T(s, W3qT if s[2] == "Q" else W3kT, c, x3T, "b_o0", "b_o1")
                    elif s in ("c_V0", "c_V1"):
                        project(s, x3T, [U * c, U * c + 1], W3vT, D)
                    elif s in ("c_xr0", "c_xr1"):
                        turn_in(s, [x3T[:, k, U * c + g, :] for g in range(U) for k in range(C)])
                    elif s in ("c_O0", "c_O1"):
                        project(s, oT, [U * c, U * c + 1], W3oT, D, f"C_out{U * c}", f"C_out{U * c + 1}")
            steps(eng, work)


_INS = ['x', 'adj', 'L0_gnn_W_q', 'L0_gnn_b_q', 'L0_gnn_W_k', 'L0_gnn_b_k', 'L0_gnn_W_v', 'L0_gnn_b_v',
        'L0_gnn_w_g', 'L0_gnn_b_g', 'L1_gnn_Wq', 'L1_gnn_bq', 'L1_gnn_Wk', 'L1_gnn_bk', 'L1_gnn_Wc',
        'L1_gnn_gamma', 'L1_gnn_beta', 'L2_gnn_fc_w', 'L2_gnn_fc_b', 'L2_gnn_q_w', 'L2_gnn_q_b',
        'L2_gnn_k_w', 'L2_gnn_k_b', 'L3_gnn_Wq', 'L3_gnn_bq', 'L3_gnn_Wk', 'L3_gnn_bk', 'L3_gnn_Wv',
        'L3_gnn_bv', 'L3_gnn_Wo', 'L3_gnn_bo', 'L3_gnn_gamma', 'L3_gnn_beta']


def kernel(**inputs):
    import numpy as _np
    import concourse.bacc as _bacc
    from concourse import mybir as _mybir
    from concourse.bass_utils import run_bass_kernel_spmd as _run

    nc = _bacc.Bacc("TRN2", target_bir_lowering=False, num_devices=1)
    arrays, args = {}, []
    for name in _INS:
        a = _np.ascontiguousarray(inputs[name])
        a = a.reshape(a.shape or (1,))
        arrays[f"in_{name}_dram"] = a
        args.append(nc.dram_tensor(f"in_{name}_dram", a.shape, _mybir.dt.from_np(a.dtype), kind="ExternalInput").ap())
    shape = _np.asarray(inputs["x"]).shape
    out = nc.dram_tensor("out_0_dram", shape, _mybir.dt.float32, kind="ExternalOutput").ap()
    gnn_kernel(nc, *args, out)
    r = _run(nc, [arrays], core_ids=[0])
    return r.results[0]["out_0_dram"]
```

```python
from contextlib import ExitStack

import concourse.bass as bass
from concourse import mybir

P = 128
D = 256
C = D // P
H = 8
R = 4
HD = D // H
G = 4
U = 2
BANK = 512

LN_EPS = 1e-5
LOG_EPS = 1e-9
ADJ_MIN = 1e-8
MASKED1 = 1e18
MASKED2 = 1e9
LEAK = 0.01

TILES = G * C

ORDERS = {
    "SA": """
        a_xT1 a_split1 a_xT0 a_split0 a_AT a_V0 a_V3 a_V1 a_V2 a_K0 a_Q0 a_cols a_rows a_K1 a_Q1
        A_score0 A_score1 A_exp0 A_turn0 s_W1kT1 A_exp1 s_W1kT0 s_W3oT0 s_W2T0 A_score2 s_W3oT1
        A_turn1 A_exp2 A_score3 s_W3kT1 A_turn2 A_score4 A_exp3 A_turn3 s_W3kT0 s_W1qT0 s_W3qT1
        s_wqk2 A_score5 A_exp4 s_W2T1 A_exp5 A_out0 A_turn4 A_turn5 A_score6 s_r1 A_score7 A_exp6
        s_cqk2 s_W3vT0 A_out1 A_turn6 A_exp7 A_turn7 s_W1qT1 A_out2 A_out3 s_W1qk0 s_v1 s_W3qT0 s_u1
        s_bo3 s_W1qk1 s_W3vT1""",
    "AB": """
        b_split0 b_split1 b_t0 a_xT0 b_mask b_distant b_y3 a_xT1 b_xr0 b_y1 a_split1 b_t1 b_xr1
        a_split0 b_y2 b_y0 b_S a_K0 b_exp1 b_p1 a_V0 a_V1 a_V2 a_Q0 a_V3 a_AT a_cols b_PT a_K1
        a_rows b_ctx0 b_ctx1 b_st1 A_score0 a_Q1 b_rs1 A_exp0 b_nw1 A_score1 b_zn1 A_turn0 A_score2
        c_AT A_exp1 A_exp2 b_xT0 b_xT1 A_turn1 A_score3 b_msplit0 A_exp3 A_turn2 A_out0 b_msplit1
        A_score4 A_turn3 A_score5 A_exp4 b_f3 b_f0 b_f2 b_f1 b_qk A_exp5 b_kb b_exp2 A_turn4
        A_score6 b_p2 A_turn5 A_score7 A_out1 b_P2T A_exp6 A_exp7 b_o0 b_o1 c_split0 A_turn6 A_turn7
        c_split1 A_out2 A_out3 c_K0 c_Q0 c_K1 c_Q1 c_V1 c_V0 c_made c_xr0 c_xr1 c_rows""",
    "ABC": """
        C_score0 b_split0 b_split1 b_mask C_exp0 C_score1 a_xT0 b_xr0 C_exp1 b_xr1 a_xT1 C_turn0
        C_score2 b_t1 a_split1 b_y0 b_y1 a_split0 b_t0 b_y2 b_y3 b_distant C_exp2 b_S a_V3 C_turn1
        C_score3 a_V1 C_turn2 b_exp1 C_exp3 a_K1 b_p1 C_score4 C_out0 C_turn3 b_PT a_K0 C_score5
        C_exp4 b_ctx1 C_exp5 b_ctx0 a_Q1 b_st1 a_V0 b_rs1 a_AT b_nw1 C_turn4 a_V2 b_zn1 C_score6
        C_exp6 a_cols C_turn5 a_Q0 C_score7 a_rows b_xT1 C_out1 C_turn6 b_msplit1 C_exp7 b_xT0
        A_score0 C_turn7 C_out2 A_score1 b_msplit0 A_exp0 c_osplit0 b_f0 A_exp1 b_f2 A_turn0 C_out3
        b_f3 b_f1 b_qk A_turn1 A_score2 b_kb A_exp2 c_O0 A_score3 b_exp2 A_turn2 b_p2 A_score4
        A_exp3 A_out0 A_turn3 c_osplit1 b_P2T A_score5 A_exp4 A_exp5 b_o1 A_turn4 c_O1 b_o0 A_score6
        c_st3 A_turn5 c_split1 c_split0 A_exp6 c_rs3 A_score7 A_exp7 A_out1 c_V0 c_nw3 A_turn6 c_K1
        c_zn3 c_Q1 A_turn7 A_out2 c_K0 A_out3 c_last c_Q0 c_V1 c_xr0 c_xr1 c_AT c_rows c_made""",
    "BC": """
        b_split1 b_split0 C_score0 C_score1 C_exp0 b_xr0 b_xr1 C_exp1 b_mask C_turn0 C_score2 b_y2
        b_y0 b_distant b_t0 b_t1 b_y1 b_y3 C_exp2 b_S C_turn1 b_exp1 C_turn2 b_p1 C_score3 C_score4
        C_out0 b_PT C_exp3 b_ctx1 b_ctx0 b_st1 C_exp4 C_turn3 b_rs1 b_nw1 C_score5 b_zn1 C_out1
        C_exp5 C_turn4 b_xT0 b_msplit0 b_xT1 C_turn5 b_msplit1 C_score6 C_exp6 C_out2 C_score7 b_f3
        b_f1 b_f0 b_f2 b_qk C_turn6 c_osplit0 C_exp7 b_kb C_turn7 c_O0 b_exp2 b_p2 C_out3 b_P2T
        c_osplit1 b_o0 b_o1 c_AT c_O1 c_split0 c_xr1 c_split1 c_st3 c_xr0 c_K0 c_V0 c_K1 c_rs3 c_Q0
        c_Q1 c_V1 c_nw3 c_made c_zn3 c_last c_rows""",
    "C": """
        C_score0 C_exp0 C_score1 C_exp1 C_turn0 C_score2 C_turn1 C_exp2 C_score3 C_exp3 C_turn2
        C_score4 C_exp4 C_turn3 C_score5 C_out0 C_turn4 C_score6 C_exp5 C_exp6 C_turn5 C_score7
        C_out1 C_turn6 C_exp7 c_osplit0 C_turn7 C_out2 C_out3 c_O0 c_osplit1 c_O1 c_st3 c_rs3 c_nw3
        c_zn3 c_last""",
}
NO_BANK = {"score", "exp", "turn", "split", "msplit", "osplit", "cols", "mask", "distant", "p", "qk", "st", "rs", "nw",
           "zn", "made", "c_rows", "last"}
BANKS = 4
STATION = {"c_s": "B", "c_m": "B", "c_ro": "B", "c_Q": "B", "c_K": "B", "c_V": "B", "c_A": "B", "c_x": "B",
           "c_st": "C"}
SETUP = ["s_W1qT0", "s_W1qT1", "s_W1kT0", "s_W1kT1", "s_W2T0", "s_W2T1", "s_W3qT0", "s_W3qT1", "s_W3kT0",
         "s_W3kT1", "s_W3vT0", "s_W3vT1", "s_W3oT0", "s_W3oT1", "s_W1qk0", "s_W1qk1", "s_u1", "s_v1", "s_r1",
         "s_wqk2", "s_cqk2", "s_bo3"]


def station(s):
    return STATION.get(s[:4], STATION.get(s[:3], s[0].upper()))


class Step:

    def __init__(self, stations, t, before):
        self.stations = stations
        self.order = ORDERS[stations].split()
        self.quad = {"A": t, "B": t - 1, "C": t - 2}
        jobs = [s for s in self.order if s[2:].rstrip("0123456789") not in NO_BANK and s not in NO_BANK]
        self.tiled = [s[0] for s in self.order if s.endswith("_score0")]
        self.place = {j: (n % BANKS, n // BANKS + 1) for n, j in enumerate(jobs)}
        self.jobs = [len(range(b, len(jobs), BANKS)) for b in range(BANKS)]
        self.before = before

    def after(self, steps=1):
        jobs, tiles = self.before
        return ([n + steps * m for n, m in zip(jobs, self.jobs)], tiles + steps * TILES * len(self.tiled))

    def turn(self, job):
        bank, n = self.place[job]
        return bank, self.before[0][bank] + n

    def turns(self, jobs):
        last = {}
        for job in jobs:
            bank, n = self.place[job]
            last[bank] = max(n, last.get(bank, 0))
        return [(bank, self.before[0][bank] + n) for bank, n in last.items()]

    def tile(self, station, n):
        return self.before[1] + TILES * self.tiled.index(station) + n


def gnn_kernel(nc, x, adj, L0_W_q, L0_b_q, L0_W_k, L0_b_k, L0_W_v, L0_b_v, L0_w_g, L0_b_g,
               L1_Wq, L1_bq, L1_Wk, L1_bk, L1_Wc, L1_gamma, L1_beta,
               L2_fc_w, L2_fc_b, L2_q_w, L2_q_b, L2_k_w, L2_k_b,
               L3_Wq, L3_bq, L3_Wk, L3_bk, L3_Wv, L3_bv, L3_Wo, L3_bo, L3_gamma, L3_beta, out):
    fp32, fp32r = mybir.dt.float32, mybir.dt.float32r
    ALU, ACT, AX = mybir.AluOpType, mybir.ActivationFunctionType, mybir.AxisListType
    QUADS = x.shape[0] // G
    SCALE = float(HD) ** -0.5
    SCALE1 = float(D) ** -0.5

    ctx = ExitStack()
    with ctx:
        def sb(name, shape, dt=fp32):
            return ctx.enter_context(nc.sbuf_tensor(name, shape, dt))

        def sem(name):
            return ctx.enter_context(nc.semaphore(name))

        psum = ctx.enter_context(nc.psum_tensor("psum", [P, 8 * BANK], fp32))
        bank = lambda n: psum[:, n * BANK:(n + 1) * BANK]
        scores = [bank(n).rearrange("p (r j) -> p r j", r=R) for n in range(2)]
        turned = [bank(2 + n).rearrange("p (r i) -> p r i", r=R) for n in range(2)]
        general = [bank(4 + n) for n in range(BANKS)]

        ident = sb("ident", [P, P])
        ones = sb("ones", [P, HD])
        as_rows = lambda w: w.rearrange("(c p) n -> p c n", p=P)
        as_cols = lambda b: b.rearrange("(c p) -> p c", p=P)
        spread = lambda b: b.rearrange("(a n) -> a n", a=1).broadcast_to([P, b.shape[0]])

        z1, zn1, z3, zn3, o3 = (sb(n, [P, G, D]) for n in ("z1", "zn1", "z3", "zn3", "o3"))
        raw = lambda t, n: t[:, C * n:C * (n + 1), :]

        v3 = sb("v3", [P, G, D])
        W0q, W0k = raw(z1, 1), raw(v3, 0)
        x1r, x3r = sb("x1r", [P, G, D]), sb("x3r", [P, G, D])
        wide = lambda t: t[:, :, :].rearrange("p g d -> p (g d)")[:, 0:C * (D + 2)].rearrange("p (c n) -> p c n", c=C)
        W0v = wide(x1r)
        split = lambda name, n=D: [sb(f"{name}_{part}", [P, C, n], fp32r) for part in ("hi", "lo")]
        W0v_split = split("W0v", D + 2)
        W0q_split, W0k_split = split("W0q"), split("W0k")
        b0q, b0k, b0v, b0g = sb("b0q", [P, C]), sb("b0k", [P, C]), sb("b0v", [P, C]), sb("b0g", [P, 1])
        b0q_scaled = sb("b0q_scaled", [P, C])
        W1q, W1k, W1qT, W1kT = raw(z3, 0), raw(z3, 1), raw(zn1, 0), raw(zn1, 1)
        W1qk_split = split("W1qk")
        W1c = wide(x3r)
        W1c_split = split("W1c", D + 2)
        b1q, b1k = sb("b1q", [P, C]), sb("b1k", [P, C])
        u1 = sb("u1", [P, C])
        r1 = sb("r1", [P, 1])
        g1, be1 = sb("g1", [P, C]), sb("be1", [P, C])
        W2 = raw(zn3, 0)
        W2T_split = split("W2T", D + 2)
        b2, qk2 = sb("b2", [P, C]), sb("qk2", [P, C, 2])
        qkb2, cqk2 = sb("qkb2", [P, 2]), sb("cqk2", [P, 2])
        W3q, W3k, W3v, W3o = raw(zn3, 1), raw(o3, 0), raw(o3, 1), raw(z1, 0)
        W3v_split, W3o_split = split("W3vT"), split("W3oT")
        W3oT = raw(v3, 1)
        W3q_split, W3k_split = split("W3qT"), split("W3kT")
        b3q, b3k, b3v = sb("b3q", [P, C]), sb("b3k", [P, C]), sb("b3v", [P, C])
        b3q_scaled = sb("b3q_scaled", [P, C])
        b3o = sb("b3o", [P, D])
        g3, be3 = sb("g3", [P, D]), sb("be3", [P, D])

        WEIGHTS0 = [
            (W0v[:, :, 0:D], as_rows(L0_W_v)), (W0q[:, :, :], as_rows(L0_W_q)), (W0k[:, :, :], as_rows(L0_W_k)),
            (W0v[:, :, D], as_cols(L0_w_g[0:D])), (W0v[:, :, D + 1], as_cols(L0_w_g[D:2 * D])),
            (b0q[:, :], as_cols(L0_b_q)), (b0k[:, :], as_cols(L0_b_k)), (b0v[:, :], as_cols(L0_b_v)),
            (b0g[:, :], spread(L0_b_g)),
        ]
        WEIGHTS = [
            (W1q[:, :, :], as_rows(L1_Wq)), (W1k[:, :, :], as_rows(L1_Wk)), (W1c[:, :, 0:D], as_rows(L1_Wc)),
            (b1q[:, :], as_cols(L1_bq)), (b1k[:, :], as_cols(L1_bk)),
            (g1[:, :], as_cols(L1_gamma)), (be1[:, :], as_cols(L1_beta)),
            (W2[:, :, :], as_rows(L2_fc_w)), (b2[:, :], as_cols(L2_fc_b)),
            (qk2[:, :, 0], as_cols(L2_q_w.rearrange("a n -> (a n)"))),
            (qk2[:, :, 1], as_cols(L2_k_w.rearrange("a n -> (a n)"))),
            (qkb2[:, 0:1], spread(L2_q_b)), (qkb2[:, 1:2], spread(L2_k_b)),
            (W3q[:, :, :], as_rows(L3_Wq)), (W3k[:, :, :], as_rows(L3_Wk)), (W3v[:, :, :], as_rows(L3_Wv)),
            (W3o[:, :, :], as_rows(L3_Wo)),
            (b3q[:, :], as_cols(L3_bq)), (b3k[:, :], as_cols(L3_bk)), (b3v[:, :], as_cols(L3_bv)),
            (b3o[:, :], spread(L3_bo)), (g3[:, :], spread(L3_gamma)), (be3[:, :], spread(L3_beta)),
        ]

        x_in = sb("x_in", [P, G, D])
        adjA = sb("adjA", [P, G, P])
        xT = sb("xT", [P, C, G, P])
        x_split = [sb(f"xT_{part}", [P, C, G, P], fp32r) for part in ("hi", "lo")]
        wT0 = sb("wT0", [P, G, P])
        qT0 = sb("qT0", [P, C, G, P])
        kD0 = sb("kD0", [P, C, G, R, P])
        v0 = sb("v0", [P, G, D + 2])
        ac = sb("ac", [P, G, 2])
        ac_hi = sb("ac_hi", [P, G, 2], fp32r)
        ac_lo = sb("ac_lo", [P, G, 2])
        cols = sb("cols", [P, G, P])
        rows = [sb("rows_i", [4, G, P], fp32r), sb("rows_j", [4, G, P], fp32r)]
        x1T = sb("x1T", [P, C, G, P])
        adjB = sb("adjB", [P, G, P])
        edge = sb("edge", [P, G, P])
        far1, far2 = sb("far1", [P, G, P]), adjB
        x13_split = [sb(f"x13T_{part}", [P, C, G, P], fp32r) for part in ("hi", "lo")]
        tT = sb("tT", [P, C, G, P])
        y1 = sb("y1", [P, G, D + 2])
        rr1 = sb("rr1", [P, G])
        s1, p1T = sb("s1", [P, G, P]), sb("p1T", [P, G, P])
        e1 = p1 = s1
        nm1, sum1, rs1 = sb("nm1", [P, G]), sb("sum1", [P, G]), sb("rs1", [P, G])
        x2T = sb("x2T", [P, C, G, P])
        qk = sb("qk", [P, G, 2])
        m2, f2 = tT[:, 0], y1
        s2, e2, p2, p2T = s1, e1, p1, p1T
        nm2, sum2, rs2 = sb("nm2", [P, G]), sb("sum2", [P, G]), sb("rs2", [P, G])
        x3T = sb("x3T", [P, C, G, P])
        adjC = sb("adjC", [P, G, P])
        wT3 = sb("wT3", [P, G, P])
        qT3, kD3 = sb("qT3", [P, C, G, P]), sb("kD3", [P, C, G, R, P])
        oT = sb("oT", [P, C, G, P])
        negmax = sb("negmax", [P, 2, R])
        expS = sb("expS", [P, 2, R, P])
        pT = sb("pT", [P, R, 2 * C, P])
        rinv = sb("rinv", [P, C, P])
        onorm = sb("onorm", [P, C, P])
        stats = {n: sb(f"stats{n}", [P, G, 6]) for n in "13"}
        mv = {n: sb(f"mv{n}", [P, G, 2]) for n in "13"}
        lnv, rst0, rst1, rst2, rstd, nmr = ({n: sb(f"{k}{n}", [P, G]) for n in "13"}
                                            for k in ("lnv", "rsta", "rstb", "rstc", "rstd", "nmr"))
        eps_col = sb("eps_col", [P, 1])

        weights0_in = sem("weights0_in")
        weights_in = sem("weights_in")
        ident_done = sem("ident_done")
        const_done = sem("const_done")
        zeros_done = sem("zeros_done")
        whole = lambda t, c: t[:, c]
        pair = lambda t, u: t[:, :, U * u:U * u + U, :]
        SPLITS = {"a_split": (x_split, xT, whole), "b_split": (x13_split, x1T, whole),
                  "b_msplit": (x13_split, x2T, whole), "c_split": (x13_split, x3T, whole),
                  "c_osplit": (x_split, oT, pair)}
        rounded = {n: sem(f"rounded_{n}") for n in SPLITS}
        split_done = {n: sem(f"done_{n}") for n in SPLITS}
        x_loaded, adjA_loaded, adjB_loaded, adjC_loaded = (sem(n) for n in ("x_in_s", "adjA_s", "adjB_s", "adjC_s"))
        stored = sem("stored")
        full = [sem(f"full{b}") for b in range(BANKS)]
        taken = [sem(f"taken{b}") for b in range(BANKS)]
        scored = sem("scored")
        negmaxed = sem("negmaxed")
        exped = sem("exped")
        t_full = sem("t_full")
        t_taken = sem("t_taken")
        cols_done = sem("cols_done")
        x1_done = sem("x1_done")
        edge_done, far_done = sem("edge_done"), sem("far_done")
        x3r_done = sem("x3r_done")
        proj3_done = sem("proj3_done")
        wT3_done = sem("wT3_done")
        negmax1, exp1, p1_done = sem("negmax1"), sem("exp1"), sem("p1_done")
        negmax2, exp2, p2_done, qk_done = sem("negmax2"), sem("exp2"), sem("p2_done"), sem("qk_done")
        var_done = {n: sem(f"var_done{n}") for n in "13"}
        rst_done = {n: sem(f"rst_done{n}") for n in "13"}
        norm_done = {n: sem(f"norm_done{n}") for n in "13"}
        zn_done = {n: sem(f"zn_done{n}") for n in "13"}
        chain = {n: sem(f"dve_chain{n}") for n in "ABC"}
        act_chain = {n: sem(f"act_chain{n}") for n in "13"}
        pool_chain = sem("pool_chain")
        halved = sem("halved")
        wqk_hi = sem("wqk_hi")
        W1c_chain = sem("W1c_chain")
        passed = sem("passed")
        out_ready = sem("out_ready")

        def need(eng, s, v):
            if not (isinstance(v, int) and v <= 0):
                eng.wait_ge(s, v)

        first = Step("SA", 0, ([0] * BANKS, 0))
        second = Step("AB", 1, first.after())
        STEADY = QUADS - 2

        def steps(eng, emit):
            emit(first)
            emit(second)
            base = second.after()
            probe = Step("ABC", 2, base)
            with eng.Fori(0, STEADY) as n:
                jobs = [b + n * m for b, m in zip(base[0], probe.jobs)]
                emit(Step("ABC", n + 2, (jobs, base[1] + n * TILES * len(probe.tiled))))
            late = Step("BC", QUADS, probe.after(STEADY))
            emit(late)
            emit(Step("C", QUADS + 1, late.after()))

        LINKS = {"A": 2 + G, "B": 9, "C": 5 + G}
        transposed = {"W1qT": (W1q, W1qT), "W1kT": (W1k, W1kT), "W2T": (W2, None), "W3qT": (W3q, None),
                      "W3kT": (W3k, None), "W3vT": (W3v, None), "W3oT": (W3o, None)}

        def settle(eng, step):
            eng.wait_ge(weights_in, 16 * len(WEIGHTS))
            for b, n in step.turns(SETUP):
                eng.wait_ge(taken[b], n)

        block = ctx.enter_context(nc.Block())

        @block.sync
        def _(eng):
            graphs = x.rearrange("b p d -> p b d")
            edges = adj.rearrange("b i j -> i b j")

            def quad(view, q):
                return view[:, bass.ds(q * G, G), :]

            def transfers(step):
                if "A" in step.stations:
                    q = step.quad["A"]
                    need(eng, cols_done, q)
                    eng.dma_start(x_in[:, :, :], quad(graphs, q)).then_inc(x_loaded, 16)
                    eng.dma_start(adjA[:, :, :], quad(edges, q)).then_inc(adjA_loaded, 16)
                if "S" in step.stations:
                    for dst, src in WEIGHTS0[1::2]:
                        eng.dma_start(dst, src, allow_slow_non_contiguous=True).then_inc(weights0_in, 16)
                    for dst, src in WEIGHTS:
                        eng.dma_start(dst, src, allow_slow_non_contiguous=True).then_inc(weights_in, 16)
                if "B" in step.stations:
                    q = step.quad["B"]
                    need(eng, negmax2, q)
                    eng.dma_start(adjB[:, :, :], quad(edges, q)).then_inc(adjB_loaded, 16)
                    need(eng, wT3_done, q)
                    eng.dma_start(adjC[:, :, :], quad(edges, q)).then_inc(adjC_loaded, 16)
            steps(eng, transfers)

        @block.gpsimd
        def _(eng):
            eng.memset(ident[:, :], 0.0).then_inc(pool_chain, 1)
            eng.wait_ge(pool_chain, 1)
            eng.affine_select(out=ident[:, :], in_=ident[:, :], compare_op=ALU.not_equal, fill=1.0,
                              base=0, pattern=[[-1, P]], channel_multiplier=1).then_inc(ident_done, 1)
            eng.memset(kD0[:, :, :, :, :], 0.0).then_inc(zeros_done, 1)

            def low(step, s):
                (hi, lo), src, piece = SPLITS[s[:-1]]
                before = [o for o in step.order[:step.order.index(s)] if o[:-1] == s[:-1]]
                eng.wait_ge(rounded[s[:-1]], 2 * step.quad[station(s)] + len(before) + 1)
                eng.sem_inc(passed, 1)
                c = int(s[-1])
                eng.tensor_tensor(piece(lo, c), piece(src, c), piece(hi, c).bitcast(fp32), ALU.subtract)\
                   .then_inc(split_done[s[:-1]], 1)

            def work(step):
                qA, qB, qC = (step.quad[st] for st in "ABC")
                for s in step.order:
                    c = int(s[-1]) if s[-1].isdigit() else 0
                    if s == "b_distant":
                        eng.wait_ge(edge_done, qB + 1)
                        eng.wait_ge(adjB_loaded, 16 * (qB + 1))
                        eng.sem_inc(passed, 1)
                        eng.tensor_scalar(far1[:, :, :], edge[:, :, :], -1.0, MASKED1, ALU.add, ALU.mult)\
                           .then_inc(far_done, 1)
                        eng.tensor_scalar(far2[:, :, :], adjB[:, :, :], -1.0, MASKED2, ALU.add, ALU.mult)\
                           .then_inc(far_done, 1)
                    elif s[:-1] in SPLITS:
                        low(step, s)
                    elif s == "c_last":
                        if step.stations != "C":
                            eng.wait_ge(zn_done["3"], qC + 1)
                            need(eng, stored, 16 * qC)
                            eng.sem_inc(passed, 1)
                            eng.tensor_tensor(o3[:, :, :], zn3[:, :, :], g3[:, :].unsqueeze(1).broadcast_to([P, G, D]),
                                              ALU.mult).then_inc(pool_chain, 1)
                            eng.wait_ge(pool_chain, qC + 2)
                            eng.tensor_tensor(o3[:, :, :], o3[:, :, :], be3[:, :].unsqueeze(1).broadcast_to([P, G, D]),
                                              ALU.add).then_inc(out_ready, 1)
                        eng.wait_ge(out_ready, qC + 1)
                        eng.sem_inc(passed, 1)
                        eng.dma_start(results[:, bass.ds(qC * G, G), :], o3[:, :, :]).then_inc(stored, 16)
                if "S" in step.stations:
                    eng.memset(kD3[:, :, :, :, :], 0.0).then_inc(zeros_done, 1)
                    eng.wait_ge(weights_in, 16 * len(WEIGHTS))
            results = out.rearrange("b p d -> p b d")
            steps(eng, work)
            eng.wait_ge(stored, 16 * QUADS)

        @block.scalar
        def _(eng):
            eng.preload_act_table_set("natural_log_exp_and_others")
            for dst, src in WEIGHTS0[::2]:
                eng.dma_start(dst, src, allow_slow_non_contiguous=True).then_inc(weights0_in, 16)
            act = eng.activation

            def take(step, job, ins_of):
                b, n = step.turn(job)
                eng.wait_ge(full[b], n)
                ins_of(general[b]).then_inc(taken[b], 1)

            def ready(step, *jobs):
                for b, n in step.turns(jobs):
                    eng.wait_ge(taken[b], n)

            def blocks(k_blocks, c, ps, bias):
                for r in range(R):
                    lanes = slice(HD * r, HD * (r + 1))
                    last = act(k_blocks[lanes, c, :, r, :], ps[lanes, :].rearrange("p (g j) -> p g j", g=G),
                               ACT.Identity, bias=bias[lanes, c:c + 1])
                return last

            def soft(step, e, s, nm, sums, negmaxed_, exp_):
                q = step.quad["B"]
                eng.wait_ge(negmaxed_, q + 1)
                for g in range(G):
                    act(e[:, g, :], s[:, g, :], ACT.Exp, bias=nm[:, g:g + 1],
                        accum_out=sums[:, g:g + 1]).then_inc(exp_, 1)

            def estimate(step, st, k):
                q = step.quad[st]
                eng.wait_ge(var_done[k], q + 1)
                act(lnv[k][:, :], mv[k][:, :, 1], ACT.Ln).then_inc(act_chain[k], 1)
                eng.wait_ge(act_chain[k], q + 1)
                act(rst0[k][:, :], lnv[k][:, :], ACT.Exp, scale=-0.5).then_inc(rst_done[k], 1)

            def normalise(step, st, k, z, zn):
                q = step.quad[st]
                eng.wait_ge(norm_done[k], q + 1)
                if k == "3":
                    need(eng, out_ready, q)
                for g in range(G):
                    last = act(zn[:, g, :], z[:, g, :], ACT.Identity, bias=nmr[k][:, g:g + 1],
                               scale=rstd[k][:, g:g + 1])
                last.then_inc(zn_done[k], 1)

            flat = lambda t, c: t[:, c].rearrange("p g i -> p (g i)")

            def work(step):
                for s in step.order:
                    c = int(s[-1]) if s[-1].isdigit() else 0
                    if "S" in step.stations and s[:3] in ("a_A", "a_Q", "a_K"):
                        eng.wait_ge(weights0_in, 16 * len(WEIGHTS0))
                        eng.wait_ge(const_done, 1)
                    if s in ("a_xT0", "a_xT1"):
                        need(eng, x1_done, C * G * step.quad["A"])
                        take(step, s, lambda ps: act(flat(xT, c), ps, ACT.Copy))
                    elif s == "a_AT":
                        take(step, s, lambda ps: act(wT0[:, :, :].rearrange("p g i -> p (g i)"), ps, ACT.Identity,
                                                     bias=eps_col[:, 0:1]))
                    elif s in ("a_Q0", "a_Q1"):
                        take(step, s, lambda ps: act(flat(qT0, c), ps, ACT.Identity, bias=b0q_scaled[:, c:c + 1],
                                                     scale=SCALE))
                    elif s in ("a_K0", "a_K1"):
                        if "S" in step.stations:
                            eng.wait_ge(zeros_done, 1)
                        take(step, s, lambda ps: blocks(kD0, c, ps, b0k))
                    elif s[:3] == "a_V":
                        take(step, s, lambda ps: act(v0[:, c, :], ps[:, 0:D + 2], ACT.Copy))
                    elif s in ("b_xr0", "b_xr1"):
                        take(step, s, lambda ps: act(x1r[:, U * c:U * c + U, :].rearrange("p g d -> p (g d)"), ps,
                                                     ACT.Copy))
                    elif s in ("b_t0", "b_t1"):
                        take(step, s, lambda ps: act(flat(tT, c), ps, ACT.Identity, bias=u1[:, c:c + 1]))
                    elif s[:3] == "b_y":
                        take(step, s, lambda ps: act(y1[:, c, 0:D + 1], ps[:, 0:D + 1], ACT.Copy))
                    elif s[1:5] == "_exp" and s[0] in "AC":
                        n = step.tile(s[0], c)
                        eng.wait_ge(negmaxed, n + 1)
                        for r in range(R):
                            last = act(expS[:, c % 2, r, :], scores[c % 2][:, r, :], ACT.Exp,
                                       bias=negmax[:, c % 2, r:r + 1])
                        last.then_inc(exped, 1)
                    elif s[:-1] in SPLITS:
                        if s[0] == "b" and s[2] == "s":
                            eng.wait_ge(x1_done, C * G * (step.quad["B"] + 1))
                            need(eng, split_done["c_split"], 2 * step.quad["B"])
                        else:
                            ready(step, *{"a_split": (f"a_xT{c}",), "b_msplit": (f"b_xT{c}",), "c_split": (f"b_o{c}",),
                                          "c_osplit": (f"C_out{U * c}", f"C_out{U * c + 1}")}[s[:-1]])
                        (hi, lo), src, piece = SPLITS[s[:-1]]
                        act(piece(hi, c), piece(src, c), ACT.Copy).then_inc(rounded[s[:-1]], 1)
                    elif s == "b_exp1":
                        soft(step, e1, s1, nm1, sum1, negmax1, exp1)
                    elif s == "b_PT":
                        take(step, s, lambda ps: act(p1T[:, :, :].rearrange("p g i -> p (g i)"), ps, ACT.Copy))
                    elif s in ("b_rs1", "c_rs3"):
                        estimate(step, s[0].upper(), s[-1])
                    elif s == "b_zn1":
                        normalise(step, "B", "1", z1, zn1)
                    elif s in ("b_xT0", "b_xT1"):
                        take(step, s, lambda ps: act(flat(x2T, c), ps, ACT.Identity, bias=be1[:, c:c + 1],
                                                     scale=g1[:, c:c + 1]))
                    elif s[:3] == "b_f":
                        take(step, s, lambda ps: act(f2[:, c, :], ps[:, 0:D + 2], ACT.Copy))
                    elif s == "b_exp2":
                        soft(step, e2, s2, nm2, sum2, negmax2, exp2)
                    elif s == "b_P2T":
                        take(step, s, lambda ps: act(p2T[:, :, :].rearrange("p g i -> p (g i)"), ps, ACT.Copy))
                    elif s in ("c_Q0", "c_Q1"):
                        take(step, s, lambda ps: act(flat(qT3, c), ps, ACT.Identity, bias=b3q_scaled[:, c:c + 1],
                                                     scale=SCALE))
                    elif s in ("c_K0", "c_K1"):
                        take(step, s, lambda ps: blocks(kD3, c, ps, b3k))
                    elif s in ("c_V0", "c_V1"):
                        take(step, s, lambda ps: act(v3[:, U * c:U * c + U, :].rearrange("p g d -> p (g d)"), ps,
                                                     ACT.Copy))
                    elif s == "c_made":
                        ready(step, "c_Q0", "c_Q1", "c_K0", "c_K1", "c_V0", "c_V1")
                        eng.sem_inc(proj3_done, 1)
                    elif s == "c_zn3":
                        normalise(step, "C", "3", z3, zn3)
                if "S" in step.stations:
                    eng.wait_ge(zeros_done, 2)
                    settle(eng, step)
            steps(eng, work)

        @block.vector
        def _(eng):
            eng.memset(ones[:, :], 1.0)
            eng.memset(eps_col[:, :], LOG_EPS)
            eng.memset(cols[:, :, :], 1.0)
            eng.memset(W1c[:, :, D + 1:D + 2], 0.0)
            eng.wait_ge(weights0_in, 16 * len(WEIGHTS0))
            eng.tensor_scalar_mul(b0q_scaled[:, :], b0q[:, :], SCALE)
            for n, ((hi, lo), w) in enumerate(((W0v_split, W0v), (W0q_split, W0q), (W0k_split, W0k))):
                eng.tensor_copy(hi[:, :, :], w).then_inc(const_done, 1)
                eng.wait_ge(const_done, n + 1)
                ins = eng.tensor_tensor(lo[:, :, :], w, hi[:, :, :].bitcast(fp32), ALU.subtract)
            ins.then_inc(const_done, 1)

            def setup(step, s):
                b, n = step.turn(s)
                eng.wait_ge(full[b], n)
                ps, c, name = general[b], int(s[-1]), s[2:-1]
                halves = {"W1qk": (W1qk_split, SCALE1), "W3qT": (W3q_split, 1.0), "W3kT": (W3k_split, 1.0),
                          "W3vT": (W3v_split, 1.0), "W3oT": (W3o_split, 1.0), "W2T": (W2T_split, 1.0)}
                if name in halves:
                    (hi, lo), scale = halves[name]
                    if name == "W3oT":
                        eng.tensor_copy(W3oT[:, c, :], ps[:, 0:D])
                    eng.tensor_scalar_mul(hi[:, c, 0:D], ps[:, 0:D], scale).then_inc(halved, 1)
                    eng.wait_ge(halved, [h for h in step.order if h[2:-1] in halves].index(s) + 1)
                    ins = eng.scalar_tensor_tensor(out=lo[:, c, 0:D], in0=ps[:, 0:D], scalar=scale,
                                                   in1=hi[:, c, 0:D].bitcast(fp32), op0=ALU.mult, op1=ALU.subtract)
                elif name in transposed:
                    ins = eng.tensor_copy(transposed[name][1][:, c, 0:D], ps[:, 0:D])
                elif s == "s_u1":
                    ins = eng.tensor_scalar_mul(u1[:, :], ps[:, 0:C], SCALE1)
                elif s == "s_v1":
                    eng.tensor_scalar_mul(W1c[:, :, D], ps[:, 0:C], SCALE1).then_inc(W1c_chain, 1)
                    eng.wait_ge(W1c_chain, 1)
                    eng.tensor_copy(W1c_split[0][:, :, :], W1c).then_inc(W1c_chain, 1)
                    eng.wait_ge(W1c_chain, 2)
                    ins = eng.tensor_tensor(W1c_split[1][:, :, :], W1c, W1c_split[0][:, :, :].bitcast(fp32),
                                            ALU.subtract)
                elif s == "s_r1":
                    ins = eng.tensor_scalar_mul(r1[:, :], ps[:, 0:1], SCALE1)
                elif s == "s_wqk2":
                    hi, lo = (w[:, :, D:D + 2] for w in W2T_split)
                    both = ps[:, 0:2 * C].rearrange("p (c n) -> p c n", c=C)
                    eng.tensor_copy(hi, both).then_inc(wqk_hi, 1)
                    eng.wait_ge(wqk_hi, 1)
                    ins = eng.tensor_tensor(lo, both, hi.bitcast(fp32), ALU.subtract)
                elif s == "s_cqk2":
                    ins = eng.tensor_tensor(cqk2[:, :], ps[:, 0:2], qkb2[:, :], ALU.add)
                elif s == "s_bo3":
                    ins = eng.tensor_tensor(b3o[:, :], ps[:, 0:D], b3o[:, :], ALU.add)
                ins.then_inc(taken[b], 1)

            def work(step):
                links = {st: 0 for st in step.stations}

                def link(st, ins):
                    links[st] += 1
                    ins.then_inc(chain[st], 1)
                    eng.wait_ge(chain[st], LINKS[st] * step.quad[st] + links[st])

                def begin(job):
                    b, n = step.turn(job)
                    eng.wait_ge(full[b], n)
                    return b, n, general[b]

                def ready(*jobs):
                    for b, n in step.turns(jobs):
                        eng.wait_ge(taken[b], n)

                def maxima(st, n):
                    eng.wait_ge(scored, step.tile(st, n) + 1)
                    eng.reduce_max(negmax[:, n % 2, :], scores[n % 2], axis=AX.X, negate=True)\
                       .then_inc(negmaxed, 1)

                def weigh(st, n):
                    w = wT0 if st == "A" else wT3
                    if n == 0 and st == "A":
                        ready("a_AT")
                    eng.wait_ge(t_full, step.tile(st, n) + 1)
                    eng.tensor_tensor(pT[:, :, n % (2 * C), :], turned[n % 2],
                                      w[:, n // C, :].unsqueeze(1).broadcast_to([P, R, P]),
                                      ALU.mult).then_inc(t_taken, 1)

                def attended(s, st, g):
                    b, n, ps = begin(s)
                    both = ps.rearrange("p (t c i) -> p t c i", t=2, c=C)
                    outs = [o for o in step.order if o[1:5] == "_out"]
                    if s != outs[0]:
                        ready(outs[outs.index(s) - 1])
                    done = len([o for o in outs[:outs.index(s)] if o[0] == "A"])
                    if st == "A" and done:
                        eng.wait_ge(x1_done, C * (G * step.quad["A"] + done))
                    link(st, eng.reciprocal(rinv[:, :, :], both[:, 1]))
                    if st == "C":
                        eng.tensor_tensor(oT[:, :, g, :], both[:, 0], rinv[:, :, :], ALU.mult)\
                           .then_inc(taken[b], 1)
                        return
                    eng.tensor_tensor(onorm[:, :, :], both[:, 0], rinv[:, :, :], ALU.mult).then_inc(taken[b], 1)
                    eng.wait_ge(taken[b], n)
                    for c in range(C):
                        eng.scalar_tensor_tensor(out=x1T[:, c, g, :], in0=onorm[:, c, :],
                                                 scalar=b0v[:, c:c + 1], in1=xT[:, c, g, :],
                                                 op0=ALU.add, op1=ALU.add).then_inc(x1_done, 1)

                def statistics(st, k, z):
                    for g in range(G):
                        ins = eng.bn_stats(stats[k][:, g, :], z[:, g, :])
                    link(st, ins)
                    eng.sem_inc(passed, 1)
                    for g in range(G):
                        ins = eng.bn_aggr(mv[k][:, g, :], stats[k][:, g, :])
                    link(st, ins)
                    eng.tensor_scalar_add(mv[k][:, :, 1], mv[k][:, :, 1], LN_EPS).then_inc(var_done[k], 1)

                def refine(st, k):
                    q = step.quad[st]
                    eng.wait_ge(var_done[k], q + 1)
                    eng.wait_ge(rst_done[k], q + 1)
                    link(st, eng.tensor_tensor(rst1[k][:, :], rst0[k][:, :], rst0[k][:, :], ALU.mult))
                    link(st, eng.scalar_tensor_tensor(out=rst2[k][:, :], in0=rst1[k][:, :], scalar=-0.5,
                                                      in1=mv[k][:, :, 1], op0=ALU.mult, op1=ALU.mult))
                    link(st, eng.scalar_tensor_tensor(out=rstd[k][:, :], in0=rst2[k][:, :], scalar=1.5,
                                                      in1=rst0[k][:, :], op0=ALU.add, op1=ALU.mult))
                    eng.scalar_tensor_tensor(out=nmr[k][:, :], in0=mv[k][:, :, 0], scalar=-1.0,
                                             in1=rstd[k][:, :], op0=ALU.mult, op1=ALU.mult)\
                       .then_inc(norm_done[k], 1)

                for s in step.order:
                    c = int(s[-1]) if s[-1].isdigit() else 0
                    if s in SETUP:
                        eng.wait_ge(weights_in, 16 * len(WEIGHTS))
                        if s == "s_cqk2":
                            eng.tensor_scalar_mul(b3q_scaled[:, :], b3q[:, :], SCALE)
                        setup(step, s)
                    elif s == "b_mask":
                        q = step.quad["B"]
                        eng.wait_ge(adjB_loaded, 16 * (q + 1))
                        eng.tensor_scalar(edge[:, :, :], adjB[:, :, :], 0.0, None, ALU.not_equal)\
                           .then_inc(edge_done, 1)
                    elif s == "a_cols":
                        ready("a_V0", "a_V1", "a_V2", "a_V3", "a_AT")
                        eng.tensor_scalar(ac[:, :, 0], v0[:, :, D], b0g[:, 0:1], None, ALU.add)
                        link("A", eng.tensor_copy(ac[:, :, 1], v0[:, :, D + 1]))
                        link("A", eng.tensor_copy(ac_hi[:, :, :], ac[:, :, :]))
                        hi = ac_hi[:, :, :].bitcast(fp32)
                        eng.tensor_copy(cols[:, :, 2], hi[:, :, 0])
                        eng.tensor_tensor(cols[:, :, 3], ac[:, :, 0], hi[:, :, 0], ALU.subtract)
                        eng.tensor_copy(cols[:, :, HD], hi[:, :, 1])
                        eng.tensor_tensor(cols[:, :, HD + 1], ac[:, :, 1], hi[:, :, 1], ALU.subtract)\
                           .then_inc(cols_done, 1)
                    elif s == "a_rows":
                        b, n, ps = begin(s)
                        eng.tensor_copy(rows[0][:, :, :].rearrange("p g i -> p (g i)"), ps[0:4, :])
                        eng.tensor_copy(rows[1][:, :, :].rearrange("p g i -> p (g i)"), ps[HD:HD + 4, :])\
                           .then_inc(taken[b], 1)
                    elif s[2:7] == "score":
                        maxima(s[0], c)
                    elif s[2:6] == "turn":
                        weigh(s[0], c)
                    elif s[1:5] == "_out":
                        attended(s, s[0], c)
                    elif s == "b_S":
                        ready("b_y0", "b_y1", "b_y2", "b_y3")
                        link("B", eng.tensor_scalar(rr1[:, :], y1[:, :, D], r1[:, 0:1], None, ALU.add))
                        eng.wait_ge(far_done, 2 * step.quad["B"] + 2)
                        b, n, ps = begin(s)
                        for g in range(G):
                            ins = eng.scalar_tensor_tensor(out=s1[:, g, :], in0=ps[:, g * P:(g + 1) * P],
                                                           scalar=rr1[:, g:g + 1], in1=far1[:, g, :],
                                                           op0=ALU.add, op1=ALU.add)
                        ins.then_inc(taken[b], 1)
                        eng.wait_ge(taken[b], n)
                        eng.reduce_max(nm1[:, :], s1[:, :, :], axis=AX.X, negate=True).then_inc(negmax1, 1)
                    elif s == "b_p1":
                        eng.wait_ge(exp1, G * (step.quad["B"] + 1))
                        link("B", eng.reciprocal(rs1[:, :], sum1[:, :]))
                        for g in range(G):
                            ins = eng.scalar_tensor_tensor(out=p1[:, g, :], in0=e1[:, g, :], scalar=rs1[:, g:g + 1],
                                                           in1=edge[:, g, :], op0=ALU.mult, op1=ALU.mult)
                        ins.then_inc(p1_done, 1)
                    elif s in ("b_ctx0", "b_ctx1"):
                        b, n, ps = begin(s)
                        need(eng, zn_done["1"], step.quad["B"])
                        ready("b_xr0", "b_xr1")
                        eng.tensor_tensor(z1[:, U * c:U * c + U, :].rearrange("p g d -> p (g d)"), ps,
                                          x1r[:, U * c:U * c + U, :].rearrange("p g d -> p (g d)"), ALU.add)\
                           .then_inc(taken[b], 1)
                    elif s == "b_st1":
                        for b, n in step.turns(("b_ctx0", "b_ctx1")):
                            eng.wait_ge(taken[b], n)
                        statistics("B", "1", z1)
                    elif s in ("b_nw1", "c_nw3"):
                        refine(s[0].upper(), s[-1])
                    elif s == "b_qk":
                        ready("b_f0", "b_f1", "b_f2", "b_f3")
                        eng.tensor_tensor(qk[:, :, :], f2[:, :, D:D + 2],
                                          cqk2[:, :].unsqueeze(1).broadcast_to([P, G, 2]), ALU.add)\
                           .then_inc(qk_done, 1)
                    elif s == "b_kb":
                        b, n, ps = begin(s)
                        eng.wait_ge(qk_done, step.quad["B"] + 1)
                        for g in range(G):
                            ins = eng.scalar_tensor_tensor(out=m2[:, g, :], in0=ps[:, g * P:(g + 1) * P],
                                                           scalar=qk[:, g, 0:1], in1=far2[:, g, :],
                                                           op0=ALU.add, op1=ALU.add)
                        ins.then_inc(taken[b], 1)
                        eng.wait_ge(taken[b], n)
                        link("B", eng.scalar_tensor_tensor(out=s2[:, :, :], in0=m2[:, :, :], scalar=LEAK,
                                                           in1=m2[:, :, :], op0=ALU.mult, op1=ALU.max))
                        eng.reduce_max(nm2[:, :], s2[:, :, :], axis=AX.X, negate=True).then_inc(negmax2, 1)
                    elif s == "b_p2":
                        eng.wait_ge(exp2, G * (step.quad["B"] + 1))
                        link("B", eng.reciprocal(rs2[:, :], sum2[:, :]))
                        eng.tensor_tensor(p2[:, :, :], e2[:, :, :], rs2[:, :].unsqueeze(2).broadcast_to([P, G, P]),
                                          ALU.mult).then_inc(p2_done, 1)
                    elif s in ("b_o0", "b_o1"):
                        b, n, ps = begin(s)
                        eng.scalar_tensor_tensor(out=x3T[:, c].rearrange("p g i -> p (g i)"), in0=ps,
                                                 scalar=b2[:, c:c + 1],
                                                 in1=x2T[:, c].rearrange("p g i -> p (g i)"),
                                                 op0=ALU.add, op1=ALU.add).then_inc(taken[b], 1)
                    elif s == "c_AT":
                        b, n, ps = begin(s)
                        if "C" in step.stations:
                            eng.wait_ge(t_taken, step.tile("C", TILES - 1) + 1)
                        eng.tensor_scalar_max(wT3[:, :, :].rearrange("p g i -> p (g i)"), ps, ADJ_MIN)\
                           .then_inc(taken[b], 1)
                        ready(s)
                        eng.sem_inc(wT3_done, 1)
                    elif s in ("c_xr0", "c_xr1"):
                        b, n, ps = begin(s)
                        if "C" in step.stations:
                            ready("c_O0", "c_O1")
                        eng.tensor_tensor(x3r[:, U * c:U * c + U, :], ps.rearrange("p (g d) -> p g d", g=U),
                                          b3o[:, :].unsqueeze(1).broadcast_to([P, U, D]), ALU.add)\
                           .then_inc(taken[b], 1)
                    elif s == "c_rows":
                        ready("c_xr0", "c_xr1")
                        eng.sem_inc(x3r_done, 1)
                    elif s in ("c_O0", "c_O1"):
                        b, n, ps = begin(s)
                        need(eng, zn_done["3"], step.quad["C"])
                        eng.wait_ge(x3r_done, step.quad["C"] + 1)
                        eng.tensor_tensor(z3[:, U * c:U * c + U, :].rearrange("p g d -> p (g d)"), ps,
                                          x3r[:, U * c:U * c + U, :].rearrange("p g d -> p (g d)"), ALU.add)\
                           .then_inc(taken[b], 1)
                    elif s == "c_last" and step.stations == "C":
                        q = step.quad["C"]
                        eng.wait_ge(zn_done["3"], q + 1)
                        eng.wait_ge(stored, 16 * q)
                        link("C", eng.tensor_tensor(o3[:, :, :], zn3[:, :, :],
                                                    g3[:, :].unsqueeze(1).broadcast_to([P, G, D]), ALU.mult))
                        eng.tensor_tensor(o3[:, :, :], o3[:, :, :], be3[:, :].unsqueeze(1).broadcast_to([P, G, D]),
                                          ALU.add).then_inc(out_ready, 1)
                    elif s == "c_st3":
                        for b, n in step.turns(("c_O0", "c_O1")):
                            eng.wait_ge(taken[b], n)
                        statistics("C", "3", z3)
                if "S" in step.stations:
                    settle(eng, step)
                assert all(links[st] == LINKS[st] + (step.stations == "C") for st in links if st != "S")
            steps(eng, work)

        @block.tensor
        def _(eng):
            mm = eng.matmul
            eng.wait_ge(ident_done, 1)

            def work(step):
                def begin(job, *inputs):
                    b, n = step.turn(job)
                    need(eng, taken[b], n - 1)
                    for other, m in step.turns(inputs):
                        if other != b:
                            eng.wait_ge(taken[other], m)
                    return b, general[b]

                def ready(*jobs):
                    for b, n in step.turns(jobs):
                        eng.wait_ge(taken[b], n)

                def turn_in(job, parts, *inputs):
                    b, ps = begin(job, *inputs)
                    for n, part in enumerate(parts):
                        last = eng.transpose(ps[0:part.shape[-1], n * P:(n + 1) * P], part, ident[:, :])
                    last.then_inc(full[b], 1)

                def project_T(job, w, c, src):
                    b, ps = begin(job)
                    passes = [(k, i, j) for i, j in ((1, 0), (0, 1), (0, 0)) for k in range(C)]
                    for k, i, j in passes:
                        last = mm(ps, w[i][:, k, c * P:(c + 1) * P], src[j][:, k].rearrange("p g i -> p (g i)"),
                                  start=(k, i, j) == passes[0], stop=(k, i, j) == passes[-1])
                    last.then_inc(full[b], 1)

                def setup(s):
                    eng.wait_ge(weights_in, 16 * len(WEIGHTS))
                    if s in ("s_W1qk0", "s_W1qk1", "s_u1", "s_v1"):
                        ready("s_W1qT0", "s_W1qT1", "s_W1kT0", "s_W1kT1")
                    elif s == "s_bo3":
                        ready("s_W3oT0", "s_W3oT1")
                    b, ps = begin(s)
                    name, c = s[2:-1], int(s[-1])
                    for k in range(C):
                        part = slice(k * P, (k + 1) * P)
                        two = dict(start=k == 0, stop=k == C - 1)
                        if name in transposed:
                            last = eng.transpose(ps[:, part], transposed[name][0][:, k, c * P:(c + 1) * P],
                                                 ident[:, :])
                        elif name == "W1qk":
                            last = mm(ps[:, 0:D], W1qT[:, k, c * P:(c + 1) * P], W1kT[:, k, :], **two)
                        elif s == "s_r1":
                            last = mm(ps[:, 0:1], b1q[:, k:k + 1].broadcast_to([P, P]), b1k[:, k:k + 1], **two)
                        elif s == "s_cqk2":
                            last = mm(ps[:, 0:2], b2[:, k:k + 1].broadcast_to([P, P]), qk2[:, k, :], **two)
                        elif s == "s_bo3":
                            last = mm(ps[:, 0:D], b3v[:, k:k + 1].broadcast_to([P, P]), W3oT[:, k, :], **two)
                    if s in ("s_u1", "s_v1", "s_wqk2"):
                        w, bias, width = {"s_u1": (W1kT, b1q, 1), "s_v1": (W1qT, b1k, 1), "s_wqk2": (W2, qk2, 2)}[s]
                        for c in range(C):
                            for k in range(C):
                                rhs = bias[:, k, :] if width == 2 else bias[:, k:k + 1]
                                last = mm(ps[:, c * width:(c + 1) * width], w[:, k, c * P:(c + 1) * P], rhs,
                                          start=k == 0, stop=k == C - 1)
                    last.then_inc(full[b], 1)

                def project_split(job, src, graphs, w, width):
                    b, ps = begin(job)
                    passes = [(k, i, j) for i, j in ((1, 0), (0, 1), (0, 0)) for k in range(C)]
                    for n, g in enumerate(graphs):
                        for k, i, j in passes:
                            last = mm(ps[:, n * width:(n + 1) * width], src[j][:, k, g, :], w[i][:, k, 0:width],
                                      start=(k, i, j) == passes[0], stop=(k, i, j) == passes[-1])
                    last.then_inc(full[b], 1)

                def score(st, n):
                    g, c, out = n // C, n % C, bank(n % 2)
                    qT, kD = (qT0, kD0) if st == "A" else (qT3, kD3)
                    need(eng, exped, step.tile(st, n) - 1)
                    if st == "A":
                        mm(out, rows[0][:, g, :], rows[1][:, g, :].unsqueeze(1).broadcast_to([4, R, P]),
                           start=True, stop=False, skip_group_check=True)
                    mm(out, qT[:, c, g, :], kD[:, c, g].rearrange("p r j -> p (r j)"),
                       start=st == "C", stop=True, skip_group_check=True).then_inc(scored, 1)

                def turn(st, n):
                    eng.wait_ge(exped, step.tile(st, n) + 1)
                    need(eng, t_taken, step.tile(st, n) - 1)
                    for r in range(R):
                        last = eng.transpose(turned[n % 2][:, r, :], expS[:, n % 2, r, :], ident[:, :])
                    last.then_inc(t_full, 1)

                def attend(s, st, g):
                    v = v0 if st == "A" else v3
                    b, ps = begin(s)
                    eng.wait_ge(t_taken, step.tile(st, C * g) + C)
                    first = C * (g % 2)
                    for c in range(C):
                        for r in range(R):
                            col = c * P + HD * r
                            mm(ps[HD * r:HD * (r + 1), c * P:(c + 1) * P], v[:, g, col:col + HD],
                               pT[:, r, first + c, :], start=True, stop=True)
                    for r in range(R):
                        last = mm(ps[HD * r:HD * (r + 1), C * P:2 * C * P], ones[:, :],
                                  pT[:, r, first:first + C, :].rearrange("p c i -> p (c i)"),
                                  start=True, stop=True)
                    last.then_inc(full[b], 1)

                qA, qB, qC = (step.quad[st] for st in "ABC")
                for s in step.order:
                    c = int(s[-1]) if s[-1].isdigit() else 0
                    chunk = slice(c * P, (c + 1) * P)
                    if s in SETUP:
                        setup(s)
                    elif s[:3] == "a_x":
                        eng.wait_ge(x_loaded, 16 * (qA + 1))
                        turn_in(s, [x_in[:, g, chunk] for g in range(G)])
                    elif s == "a_AT":
                        eng.wait_ge(adjA_loaded, 16 * (qA + 1))
                        turn_in(s, [adjA[:, g, :] for g in range(G)])
                    elif s in ("a_Q0", "a_Q1", "a_K0", "a_K1"):
                        eng.wait_ge(split_done["a_split"], 2 * (qA + 1))
                        if "S" in step.stations:
                            eng.wait_ge(const_done, 3 if s[2] == "Q" else 4)
                        project_T(s, W0q_split if s[2] == "Q" else W0k_split, c, x_split)
                    elif s[:3] == "a_V":
                        eng.wait_ge(split_done["a_split"], 2 * (qA + 1))
                        if "S" in step.stations:
                            eng.wait_ge(const_done, 2)
                        project_split(s, x_split, [c], W0v_split, D + 2)
                    elif s == "a_rows":
                        eng.wait_ge(cols_done, qA + 1)
                        turn_in(s, [cols[:, g, :] for g in range(G)])
                    elif s[2:7] == "score":
                        if s == "A_score0":
                            ready("a_Q0", "a_K0", "a_rows")
                        elif s == "A_score1":
                            ready("a_Q1", "a_K1")
                        elif s == "C_score0":
                            eng.wait_ge(proj3_done, qC + 1)
                        score(s[0], c)
                    elif s[2:6] == "turn":
                        turn(s[0], c)
                    elif s[1:5] == "_out":
                        if s == "A_out0":
                            ready("a_V0", "a_V1", "a_V2", "a_V3")
                        attend(s, s[0], c)
                    elif s in ("b_xr0", "b_xr1"):
                        eng.wait_ge(x1_done, C * G * (qB + 1))
                        turn_in(s, [x1T[:, k, U * c + g, :] for g in range(U) for k in range(C)])
                    elif s in ("b_t0", "b_t1"):
                        eng.wait_ge(split_done["b_split"], 2 * (qB + 1))
                        project_T(s, W1qk_split, c, x13_split)
                    elif s[:3] == "b_y":
                        eng.wait_ge(split_done["b_split"], 2 * (qB + 1))
                        project_split(s, x13_split, [c], W1c_split, D + 2)
                    elif s == "b_S":
                        b, ps = begin(s, "b_t0", "b_t1")
                        for g in range(G):
                            for k in range(C):
                                last = mm(ps[:, g * P:(g + 1) * P], tT[:, k, g, :], x1T[:, k, g, :],
                                          start=k == 0, stop=k == C - 1)
                        last.then_inc(full[b], 1)
                    elif s == "b_PT":
                        eng.wait_ge(p1_done, qB + 1)
                        turn_in(s, [p1[:, g, :] for g in range(G)])
                    elif s in ("b_ctx0", "b_ctx1"):
                        b, ps = begin(s, "b_PT", f"b_y{U * c}", f"b_y{U * c + 1}")
                        for g in range(U):
                            last = mm(ps[:, g * D:(g + 1) * D], p1T[:, U * c + g, :], y1[:, U * c + g, 0:D],
                                      start=True, stop=True)
                        last.then_inc(full[b], 1)
                    elif s in ("b_xT0", "b_xT1"):
                        eng.wait_ge(zn_done["1"], qB + 1)
                        turn_in(s, [zn1[:, g, chunk] for g in range(G)])
                    elif s[:3] == "b_f":
                        eng.wait_ge(split_done["b_msplit"], 2 * (qB + 1))
                        project_split(s, x13_split, [c], W2T_split, D + 2)
                    elif s == "b_kb":
                        eng.wait_ge(qk_done, qB + 1)
                        turn_in(s, [qk[:, g, 1:2].broadcast_to([P, P]) for g in range(G)])
                    elif s == "b_P2T":
                        eng.wait_ge(p2_done, qB + 1)
                        turn_in(s, [p2[:, g, :] for g in range(G)])
                    elif s in ("b_o0", "b_o1"):
                        b, ps = begin(s, "b_P2T")
                        for g in range(G):
                            last = mm(ps[:, g * P:(g + 1) * P], f2[:, g, chunk], p2T[:, g, :], start=True, stop=True)
                        last.then_inc(full[b], 1)
                    elif s == "c_AT":
                        eng.wait_ge(adjC_loaded, 16 * (qB + 1))
                        turn_in(s, [adjC[:, g, :] for g in range(G)])
                    elif s in ("c_Q0", "c_Q1", "c_K0", "c_K1"):
                        eng.wait_ge(split_done["c_split"], 2 * (qB + 1))
                        project_T(s, W3q_split if s[2] == "Q" else W3k_split, c, x13_split)
                    elif s in ("c_V0", "c_V1"):
                        eng.wait_ge(split_done["c_split"], 2 * (qB + 1))
                        project_split(s, x13_split, [U * c, U * c + 1], W3v_split, D)
                    elif s in ("c_xr0", "c_xr1"):
                        turn_in(s, [x3T[:, k, U * c + g, :] for g in range(U) for k in range(C)], "b_o0", "b_o1")
                    elif s in ("c_O0", "c_O1"):
                        before = [o for o in step.order[:step.order.index(s)] if o[:-1] == "c_osplit"]
                        assert s.replace("O", "osplit") in before
                        eng.wait_ge(split_done["c_osplit"], 2 * qC + len(before))
                        project_split(s, x_split, [U * c, U * c + 1], W3o_split, D)
                if "S" in step.stations:
                    settle(eng, step)
            steps(eng, work)


_INS = ['x', 'adj', 'L0_gnn_W_q', 'L0_gnn_b_q', 'L0_gnn_W_k', 'L0_gnn_b_k', 'L0_gnn_W_v', 'L0_gnn_b_v',
        'L0_gnn_w_g', 'L0_gnn_b_g', 'L1_gnn_Wq', 'L1_gnn_bq', 'L1_gnn_Wk', 'L1_gnn_bk', 'L1_gnn_Wc',
        'L1_gnn_gamma', 'L1_gnn_beta', 'L2_gnn_fc_w', 'L2_gnn_fc_b', 'L2_gnn_q_w', 'L2_gnn_q_b',
        'L2_gnn_k_w', 'L2_gnn_k_b', 'L3_gnn_Wq', 'L3_gnn_bq', 'L3_gnn_Wk', 'L3_gnn_bk', 'L3_gnn_Wv',
        'L3_gnn_bv', 'L3_gnn_Wo', 'L3_gnn_bo', 'L3_gnn_gamma', 'L3_gnn_beta']


def kernel(**inputs):
    import numpy as _np
    import concourse.bacc as _bacc
    from concourse import mybir as _mybir
    from concourse.bass_utils import run_bass_kernel_spmd as _run

    nc = _bacc.Bacc("TRN2", target_bir_lowering=False, num_devices=1)
    arrays, args = {}, []
    for name in _INS:
        a = _np.ascontiguousarray(inputs[name])
        a = a.reshape(a.shape or (1,))
        arrays[f"in_{name}_dram"] = a
        args.append(nc.dram_tensor(f"in_{name}_dram", a.shape, _mybir.dt.from_np(a.dtype), kind="ExternalInput").ap())
    shape = _np.asarray(inputs["x"]).shape
    out = nc.dram_tensor("out_0_dram", shape, _mybir.dt.float32, kind="ExternalOutput").ap()
    gnn_kernel(nc, *args, out)
    r = _run(nc, [arrays], core_ids=[0])
    return r.results[0]["out_0_dram"]
```
